# Optimizing a Trainium2 kernel written in Bass

```python
import numpy as np
import jax
import jax.numpy as jnp

def _softmax(x, axis=-1):
    return jax.nn.softmax(x, axis=axis)

def _gelu(x):
    return jax.nn.gelu(x, approximate=True)

def _silu(x):
    return jax.nn.silu(x)

def _sigmoid(x):
    return jax.nn.sigmoid(x)

def _layernorm(x, axis=-1, eps=1e-05):
    m = jnp.mean(x, axis=axis, keepdims=True)
    v = jnp.var(x, axis=axis, keepdims=True)
    return (x - m) / jnp.sqrt(v + eps)

def _scatter_add(tgt, idx, src, axis=0):
    return tgt.at[idx].add(src)

def _segment_sum(src, seg, n):
    return jax.ops.segment_sum(src, seg, n)
kernel_name = 'mk_macaron_d1_jaxref_r8_d97eaf'

def setup_inputs(seed: int=0):
    np.random.seed(seed)
    _w = jnp.asarray

    def _L0_attn_setup():
        import jax, jax.numpy as jnp
        import numpy as np
        HIDDEN = 128
        TILE = 128
        key = jax.random.key(seed)
        ks = jax.random.split(key, 9)
        B, S, D = (2, 512, HIDDEN)
        s = 1.0 / np.sqrt(D)
        return {'batch': jax.random.normal(ks[0], (B, S, D), jnp.float32), 'Wq': jax.random.normal(ks[1], (D, D), jnp.float32) * s, 'bq': jax.random.normal(ks[2], (D,), jnp.float32) * 0.01, 'Wk': jax.random.normal(ks[3], (D, D), jnp.float32) * s, 'bk': jax.random.normal(ks[4], (D,), jnp.float32) * 0.01, 'Wv': jax.random.normal(ks[5], (D, D), jnp.float32) * s, 'bv': jax.random.normal(ks[6], (D,), jnp.float32) * 0.01, 'Wo': jax.random.normal(ks[7], (D, D), jnp.float32) * s, 'bo': jax.random.normal(ks[8], (D,), jnp.float32) * 0.01}
    _L0_attn_in = _L0_attn_setup()

    def _L0_ffn_setup():
        import jax, jax.numpy as jnp
        import numpy as np
        TOP_K = 2
        E = 8
        D = 128
        F = 256
        B, S = (2, 128)
        key = jax.random.key(seed)
        ks = jax.random.split(key, 8)
        sc = 0.02
        return {'x_bsD': jax.random.normal(ks[0], (B, S, D), dtype=jnp.float32), 'router_DE': jax.random.normal(ks[1], (D, E), dtype=jnp.float32) * sc, 'w_in_shared_FD': jax.random.normal(ks[2], (F, D), dtype=jnp.float32) * sc, 'w_out_shared_DF': jax.random.normal(ks[3], (D, F), dtype=jnp.float32) * sc, 'w_swiglu_FD': jax.random.normal(ks[4], (F, D), dtype=jnp.float32) * sc, 'w_in_eDF': jax.random.normal(ks[5], (E, D, F), dtype=jnp.float32) * sc, 'w_swiglu_eDF': jax.random.normal(ks[6], (E, D, F), dtype=jnp.float32) * sc, 'w_out_eFD': jax.random.normal(ks[7], (E, F, D), dtype=jnp.float32) * sc}
    _L0_ffn_in = _L0_ffn_setup()
    _d = {'L0_attn_batch': _L0_attn_in['batch'], 'L0_attn_Wq': _L0_attn_in['Wq'], 'L0_attn_bq': _L0_attn_in['bq'], 'L0_attn_Wk': _L0_attn_in['Wk'], 'L0_attn_bk': _L0_attn_in['bk'], 'L0_attn_Wv': _L0_attn_in['Wv'], 'L0_attn_bv': _L0_attn_in['bv'], 'L0_attn_Wo': _L0_attn_in['Wo'], 'L0_attn_bo': _L0_attn_in['bo'], 'L0_ffn_router_DE': _L0_ffn_in['router_DE'], 'L0_ffn_w_in_shared_FD': _L0_ffn_in['w_in_shared_FD'], 'L0_ffn_w_out_shared_DF': _L0_ffn_in['w_out_shared_DF'], 'L0_ffn_w_swiglu_FD': _L0_ffn_in['w_swiglu_FD'], 'L0_ffn_w_in_eDF': _L0_ffn_in['w_in_eDF'], 'L0_ffn_w_swiglu_eDF': _L0_ffn_in['w_swiglu_eDF'], 'L0_ffn_w_out_eFD': _L0_ffn_in['w_out_eFD']}
    _x0 = _d['L0_attn_batch']
    _d['L0_attn_batch'] = jax.random.normal(jax.random.fold_in(jax.random.key(seed), 1), (16, 512, 128), dtype=_x0.dtype)
    del _x0
    return _d

def reference(L0_attn_batch, L0_attn_Wq, L0_attn_bq, L0_attn_Wk, L0_attn_bk, L0_attn_Wv, L0_attn_bv, L0_attn_Wo, L0_attn_bo, L0_ffn_router_DE, L0_ffn_w_in_shared_FD, L0_ffn_w_out_shared_DF, L0_ffn_w_swiglu_FD, L0_ffn_w_in_eDF, L0_ffn_w_swiglu_eDF, L0_ffn_w_out_eFD):

    def _L0_attn_ref(batch, Wq, bq, Wk, bk, Wv, bv, Wo, bo):
        import jax, jax.numpy as jnp
        import numpy as np
        HIDDEN = 128
        TILE = 128
        B, S, D = batch.shape
        scale = 1.0 / np.sqrt(D)
        T = S // TILE
        q = batch @ Wq.T + bq
        k = batch @ Wk.T + bk
        v = batch @ Wv.T + bv
        k_t = k.reshape(B, T, TILE, D)
        v_t = v.reshape(B, T, TILE, D)
        scores = jnp.einsum('bqd,btkd->btqk', q, k_t) * scale
        w = jax.nn.softmax(scores, axis=-1)
        out = jnp.einsum('btqk,btkd->bqd', w, v_t)
        norm = w.sum(axis=-1).sum(axis=1)[..., None]
        out = out / (norm + 1e-06)
        return out @ Wo.T + bo

    def _L0_ffn_ref(x_bsD, router_DE, w_in_shared_FD, w_out_shared_DF, w_swiglu_FD, w_in_eDF, w_swiglu_eDF, w_out_eFD):
        import jax, jax.numpy as jnp
        import numpy as np
        TOP_K = 2
        E = 8
        D = 128
        F = 256
        B, S = (2, 128)
        b, s, d = x_bsD.shape
        x_aD = x_bsD.reshape(-1, d)
        a = x_aD.shape[0]
        scores_aE = x_aD @ router_DE
        topv_aK, topi_aK = jax.lax.top_k(scores_aE, TOP_K)
        masked_aE = jnp.full_like(scores_aE, -jnp.inf)
        masked_aE = masked_aE.at[jnp.arange(a)[:, None], topi_aK].set(topv_aK)
        gates_Ea = jax.nn.sigmoid(masked_aE.astype(jnp.float32)).astype(x_aD.dtype).T
        routed_in_EaD = x_aD[None, :, :] * gates_Ea[:, :, None]
        routed_in_EaD = jax.lax.stop_gradient(routed_in_EaD)
        mid_EaF = jnp.einsum('ead,edf->eaf', routed_in_EaD, w_in_eDF)
        sw_EaF = jnp.einsum('ead,edf->eaf', routed_in_EaD, w_swiglu_eDF)
        h_EaF = jax.nn.silu(mid_EaF) * sw_EaF
        out_EaD = jnp.einsum('eaf,efd->ead', h_EaF, w_out_eFD)
        shared_aF = jax.nn.silu(x_aD @ w_in_shared_FD.T) * (x_aD @ w_swiglu_FD.T)
        shared_out_aD = jax.lax.stop_gradient(shared_aF @ w_out_shared_DF.T)
        out_aD = shared_out_aD + jnp.sum(out_EaD, axis=0)
        return out_aD.reshape(b, s, d)
    x = L0_attn_batch
    x = x + 0.5 * _L0_ffn_ref(_layernorm(x, axis=-1), L0_ffn_router_DE, L0_ffn_w_in_shared_FD, L0_ffn_w_out_shared_DF, L0_ffn_w_swiglu_FD, L0_ffn_w_in_eDF, L0_ffn_w_swiglu_eDF, L0_ffn_w_out_eFD)
    x = x + _L0_attn_ref(_layernorm(x, axis=-1), L0_attn_Wq, L0_attn_bq, L0_attn_Wk, L0_attn_bk, L0_attn_Wv, L0_attn_bv, L0_attn_Wo, L0_attn_bo)
    x = x + 0.5 * _L0_ffn_ref(_layernorm(x, axis=-1), L0_ffn_router_DE, L0_ffn_w_in_shared_FD, L0_ffn_w_out_shared_DF, L0_ffn_w_swiglu_FD, L0_ffn_w_in_eDF, L0_ffn_w_swiglu_eDF, L0_ffn_w_out_eFD)
    return x

_drawn_inputs = setup_inputs


def setup_inputs(seed=0):
    import zlib

    import numpy as np

    out = dict(_drawn_inputs(seed))
    spreads = {}
    factors = {'L0_attn_bq': 8.0,
     'L0_attn_bk': 8.0,
     'L0_attn_bv': 5.242,
     'L0_attn_bo': 5.433,
     'L0_ffn_router_DE': 8.0,
     'L0_ffn_w_in_shared_FD': 6.836,
     'L0_ffn_w_out_shared_DF': 6.76,
     'L0_ffn_w_swiglu_FD': 6.826,
     'L0_ffn_w_in_eDF': 8.0,
     'L0_ffn_w_swiglu_eDF': 8.0,
     'L0_ffn_w_out_eFD': 8.0}
    for name, (base, spread) in spreads.items():
        noise = np.random.default_rng([zlib.crc32(name.encode()), seed]).standard_normal(out[name].shape)
        drawn = base * np.exp(spread * noise) if base else spread * noise
        out[name] = jnp.asarray(drawn.astype(out[name].dtype))
    for name, factor in factors.items():
        out[name] = (out[name] * factor).astype(out[name].dtype)
    return out
```

```python
from contextlib import ExitStack

import concourse.bass as bass
from concourse import mybir

F32 = mybir.dt.float32
F32R = mybir.dt.float32r
BF16 = mybir.dt.bfloat16
I32 = mybir.dt.int32
U32 = mybir.dt.uint32
ACT = mybir.ActivationFunctionType
ALU = mybir.AluOpType
AXX = mybir.AxisListType.X

P = 128
BT = 4
TOPK = 2
EPS = 1e-5
ds = bass.ds


class Steps:

    def __init__(self, eng, sem, n=0):
        self.eng, self.sem, self.base, self.n, self.last = eng, sem, 0, n, None

    def did(self, ins):
        ins.then_inc(self.sem, 1)
        self.n += 1
        self.last = None
        return ins

    def signals(self, ins, sem, count):
        ins.then_inc(sem, 1)
        self.last = sem, count

    def mark(self):
        return self.last or (self.sem, self.base + self.n)

    def settle(self):
        self.eng.wait_ge(*self.mark())

    def enter(self, turn, per_turn):
        self.before = self.base + self.n
        self.base, self.n = self.before + turn * per_turn, 0

    def leave(self, turns, per_turn):
        assert self.n == per_turn, f"steps in a turn of the loop: {self.n}, not {per_turn}"
        self.base, self.n = self.before + turns * per_turn, 0


class At:

    def __init__(self, i, buf, uses, total):
        self.i, self.buf, self.uses = i, buf, uses
        self.live = not isinstance(i, int) or 0 <= i < total


def rolled(eng, total, ahead, behind, body, steps=None, per_turn=0, n=2, peel=2):
    first = -(-(behind + peel) // n) * n
    turns = (total - ahead - first) // n

    def peeled(i):
        body(lambda k: At(i + k, (i + k) % n, (i + k) // n, total))

    for i in range(-ahead, first):
        peeled(i)
    with eng.Fori(0, turns) as r:
        if steps:
            steps.enter(r, per_turn)
        for u in range(n):
            body(lambda k: At(first + r * n + (u + k), (first + u + k) % n, r + (first + u + k) // n, total))
        if steps:
            steps.leave(turns, per_turn)
    for i in range(first + turns * n, total + behind):
        peeled(i)


def due(count):
    return not isinstance(count, int) or count > 0


def macaron(nc, batch, wq, bq, wk, bk, wv, bv, wo, bo, router, w_in_sh, w_out_sh, w_sw_sh,
            w_in_e, w_sw_e, w_out_e, out):
    B, S, D = batch.shape
    E, _, F = w_in_e.shape
    N = B * S
    T = N // P
    NB = T // BT
    W = BT * P
    G = S // P
    FC = F // P
    assert D == P and S == W and FC == 2 and E == 8
    CAP = N + P
    SLOTS = 8
    NT = -(-(TOPK * T + E - 1) // SLOTS) * SLOTS
    DUMMY = 8
    assert NT - TOPK * T <= DUMMY
    ROW = D + 1
    PADS = TOPK * N
    SCALE = float(D) ** -0.5

    x_t = batch.rearrange("b (j p) d -> p (b j) d", p=P)
    out_t = out.rearrange("b (j p) d -> p (b j) d", p=P)
    pairs = nc.dram_tensor("pairs", [E * CAP + DUMMY * P, ROW], F32).ap()
    results = nc.dram_tensor("results", [PADS + (E + DUMMY) * P, D], F32).ap()
    results_t = results[0:PADS, :].rearrange("(k t p) d -> p k t d", k=TOPK, p=P)

    with ExitStack() as ctx:
        def sb(name, shape, dt=F32):
            return ctx.enter_context(nc.sbuf_tensor(name, shape, dt))

        def sem(name):
            return ctx.enter_context(nc.semaphore(name))

        def sems(name, n):
            return [sem(f"{name}{i}") for i in range(n)]

        bank = [ctx.enter_context(nc.psum_tensor(f"bank{i}", [P, 512], F32)) for i in range(8)]

        X = sb("X", [P, T, D])
        XTR = sb("XTR", [P, N])
        XTH = sb("XTH", [P, 2, W], F32R)
        XTL = sb("XTL", [P, 2, W], F32R)
        WEH = sb("WEH", [P, E * 2 * F], F32R)
        WEL = sb("WEL", [P, E * 2 * F], F32R)
        WOE = sb("WOE", [P, E * FC * D])
        SHH = sb("SHH", [P, 2 * F], F32R)
        SHL = sb("SHL", [P, 2 * F], F32R)
        WOS = sb("WOS", [P, FC, D])
        WT4 = sb("WT4", [P, 4, D])
        RT = sb("RT", [P, E])
        bq_s = sb("bq_s", [P, 1])
        bk_s = sb("bk_s", [P, 1])
        bias_row = sb("bias_row", [1, 2, D])
        one_row = sb("one_row", [1, P])
        ident = sb("ident", [P, P])
        before = sb("before", [P, P], BF16)
        ones = sb("ones", [P, P], BF16)
        expert_no = sb("expert_no", [P, E])
        region = sb("region", [P, E])
        part_no = sb("part_no", [P, 1])
        dest = sb("dest", [P, TOPK, T], I32)
        pad_rows = sb("pad_rows", [P, E, ROW])
        pad_at = sb("pad_at", [P, E], U32)
        next_row = sb("next_row", [P, E])
        eps_c = sb("eps_c", [P, 1])
        ints = sb("ints", [P, E * 2], I32)
        tile_no = sb("tile_no", [1, NT])
        upto = sb("upto", [1, E, E])
        tile_i = sb("tile_i", [1, NT], I32)
        expert_of = sb("expert_of", [1, NT], I32)
        row_of = sb("row_of", [1, NT], I32)
        tcnt = sb("tcnt", [1, 4, E])
        tcnt_i = sb("tcnt_i", [1, 2, E], I32)
        tee = sb("tee", [1, E, E])
        tot_t = sb("tot_t", [1, 3, NT])
        XN = sb("XN", [P, 2, BT, D])
        XT32 = sb("XT32", [P, 2, W])
        ST = sb("ST", [P, 2, BT, 6])
        MV = sb("MV", [P, 2, BT, 2])
        MEAN = sb("MEAN", [P, T])
        VAR = sb("VAR", [P, T])
        STD = sb("STD", [P, T])
        SD = sb("SD", [P, 2, BT])
        RST = sb("RST", [P, 2, BT])
        RSTD = sb("RSTD", [P, T])
        SC = sb("SC", [P, BT, E])
        TOP = sb("TOP", [P, 2, BT, 8])
        TOPI = sb("TOPI", [P, BT, 8], U32)
        TNH = sb("TNH", [P, 2, BT, TOPK])
        GATE = sb("GATE", [P, 2, BT, TOPK])
        HOT = sb("HOT", [P, BT, TOPK, E])
        HOTB = sb("HOTB", [P, BT, E], BF16)
        RANK = sb("RANK", [P, BT, E])
        PICK = sb("PICK", [P, BT, TOPK, E])
        POS = sb("POS", [P, 2, BT, TOPK], U32)
        PAY = sb("PAY", [P, 2, TOPK, BT, ROW])
        arena = sb("arena", [P, 3584])

        def view(at, *shape):
            size = 1
            for n in shape:
                size *= n
            v = arena[:, at:at + size]
            if len(shape) == 1:
                return v
            names = "abc"[:len(shape)]
            return v.rearrange(f"p ({' '.join(names)}) -> p {' '.join(names)}", **dict(zip(names, shape)))

        XS = view(0, SLOTS, ROW)
        YO = view(SLOTS * ROW, SLOTS, D)
        SSG = view(0, FC, W)
        SHH_T = view(FC * W, FC, W)
        AN = view(0, BT, D)
        AXT = view(512, W)
        QT = view(1024, W)
        KT = view(1536, W)
        PT = view(2048, 2, W)
        OT = view(3072, W)
        SHT = view(2048, 2 * F)
        XSH = sb("XSH", [P, 2, P], F32R)
        XSL = sb("XSL", [P, 2, P], F32R)
        SG = sb("SG", [P, 2, F])
        H = sb("H", [P, 2, F])
        HT = sb("HT", [P, 2, F])
        Y2 = sb("Y2", [P, 2, TOPK, BT, D])
        big = sb("big", [P, 2, BT, W])
        V = sb("V", [P, 2, G, D])
        NM = sb("NM", [P, 2, BT, G])
        SUM = sb("SUM", [P, 2, BT, G])
        R1 = sb("R1", [P, BT, G])
        R2 = sb("R2", [P, BT, G])
        R3 = sb("R3", [P, BT, 1])
        R4 = sb("R4", [P, BT, 1])

        vec = sem("vector_steps")
        act_s = sem("scalar_steps")
        pool_s = sem("pool_steps")
        k = dict((n, sem(n)) for n in (
            "weights_loaded small_loaded prep_transposed prep_read consts table_done pads_written "
            "stats_done std_done normed xt_turned xt_copied xt_split scored topped tanh_done picked ranked "
            "rank_read gate_done pay0 pay1 placed up0 up1 silu0 silu1 hid0 hid1 down shared_added "
            "xs_turned xs_high xs_low e_up e_silu e_hid e_turned e_copied e_down e_out "
            "a_stats a_std a_normed a_turned a_copied q_made k_made v_made q_ready k_ready v_ready "
            "s_made m_ready probs_ready scaled t_even t_odd c_even c_odd av_made ot_ready proj_made updated "
            "carried_s carried_y kept_split r_stats r_std combined stored_y").split())
        x_loaded = sems("x_loaded", 2)
        y_loaded = sems("y_loaded", 2)
        scattered = sems("scattered", 2)
        xs_loaded = sems("xs_loaded", SLOTS)
        y_sent = sems("y_sent", SLOTS)
        stored = sems("stored", 2)

        def carry(dve, word=0):
            dve.memset(spare_v[:, word:word + 1], 0.0)

        def pool_carry(pool, which, n):
            if due(n):
                pool.wait_ge(k[which], n)
            word = spare_p[:, 0:1] if which == "carried_s" else spare_p[:, 1:2]
            pool.tensor_tensor(word, spare_p[:, 2:3], spare_p[:, 2:3], ALU.add).then_inc(k[which], 1)

        def x_block(b):
            return X[:, ds(BT * b.i, BT), :] if not isinstance(b.i, int) else X[:, BT * b.i:BT * b.i + BT, :]

        def cut(buf, at, size):
            return buf[:, at:at + size] if isinstance(at, int) else buf[:, ds(at, size)]

        def cols(buf, b):
            return cut(buf, BT * b.i, BT)

        def tile_of(buf, t):
            return buf[:, t:t + 1, :] if isinstance(t, int) else buf[:, ds(t, 1), :]

        def chunk(ap, j):
            return ap[:, j * P:(j + 1) * P]

        wst = view(0, 6, D)
        spare_v = sb("spare_v", [1, 5])
        spare_p = sb("spare_p", [1, 3])
        vec_at = []
        stage = big[:, :, :, :].rearrange("p a b w -> p (a b w)")

        with nc.Block() as block:
            @block.sync
            def _(sp):
                st3 = stage.rearrange("p (e g f) -> p e g f", e=E, g=2)
                sp.dma_start(st3[:, :, 0, :], w_in_e.rearrange("e d f -> d e f")).then_inc(k["weights_loaded"], 16)
                sp.dma_start(st3[:, :, 1, :], w_sw_e.rearrange("e d f -> d e f")).then_inc(k["weights_loaded"], 16)
                sp.dma_start(WOE[:, :].rearrange("p (e c d) -> p e c d", e=E, c=FC),
                             w_out_e.rearrange("e (c p) d -> p e c d", p=P)).then_inc(k["weights_loaded"], 16)
                sp.wait_ge(k["consts"], 1)
                sp.dma_start(pairs[E * CAP:E * CAP + DUMMY * P, :].rearrange("(e p) r -> p e r", p=P),
                             pad_rows[:, :, :]).then_inc(k["pads_written"], 16)
                sp.wait_ge(k["weights_loaded"], 48)
                sp.wait_ge(k["pads_written"], 16)

            @block.scalar
            def _(act):
                small = k["small_loaded"]
                act.dma_start(wst[:, 0:2, :],
                              w_in_sh.rearrange("(c p) d -> p c d", p=P)).then_inc(small, 16)
                act.dma_start(wst[:, 2:4, :], w_sw_sh.rearrange("(c p) d -> p c d", p=P)).then_inc(small, 16)
                act.dma_start(wst[:, 4:6, :].rearrange("p c d -> p (c d)"), w_out_sh).then_inc(small, 16)
                for n, w in enumerate((wq, wk, wv, wo)):
                    act.dma_start(XN[:, 0, n, :], w).then_inc(small, 16)
                act.dma_start(RT[:, :], router).then_inc(small, 16)
                act.dma_start(bq_s[:, :], bq.rearrange("(d a) -> d a", a=1)).then_inc(small, 16)
                act.dma_start(bk_s[:, :], bk.rearrange("(d a) -> d a", a=1)).then_inc(small, 16)
                act.dma_start(bias_row[:, 0, :], bv.rearrange("(a d) -> a d", a=1)).then_inc(small, 16)
                act.dma_start(bias_row[:, 1, :], bo.rearrange("(a d) -> a d", a=1)).then_inc(small, 16)
                act.wait_ge(small, 12 * 16)
                act.activation(bq_s[:, :], bq_s[:, :], ACT.Copy, scale=SCALE).then_inc(act_s, 1)

            @block.gpsimd
            def _(pool):
                st = Steps(pool, pool_s)
                for m, v in ((ident, 0.0), (before, 1.0), (ones, 1.0), (one_row, 1.0), (eps_c, EPS), (spare_p, 0.0), (pad_rows, 0.0),
                             (upto, 1.0)):
                    st.did(pool.memset(m[tuple(slice(None) for _ in m.shape)], v))
                st.did(pool.iota(ints[:, 0:E], pattern=[[P, E]], base=PADS + E * P, channel_multiplier=1))
                st.settle()
                st.did(pool.affine_select(out=ident[:, :], in_=ident[:, :], compare_op=ALU.not_equal, fill=1.0,
                                          base=0, pattern=[[-1, P]], channel_multiplier=1))
                st.did(pool.affine_select(out=before[:, :], in_=before[:, :], compare_op=ALU.is_gt, fill=0.0,
                                          base=0, pattern=[[1, P]], channel_multiplier=-1))
                st.did(pool.affine_select(out=upto[:, :, :], in_=upto[:, :, :], compare_op=ALU.is_ge, fill=0.0,
                                          base=0, pattern=[[1, E], [-1, E]], channel_multiplier=0))
                pool.tensor_copy(pad_rows[:, :, D:D + 1].bitcast(I32), ints[:, 0:E].unsqueeze(2)).then_inc(k["consts"], 1)
                st.did(pool.iota(dest[:, :, :], pattern=[[N, TOPK], [P, T]], base=0, channel_multiplier=1))
                st.did(pool.iota(tile_i[:, :], pattern=[[1, NT]], base=0, channel_multiplier=0))
                st.did(pool.iota(ints[:, E:2 * E], pattern=[[1, E]], base=0, channel_multiplier=0))
                st.settle()
                st.did(pool.tensor_copy(tile_no[:, :], tile_i[:, :]))
                st.did(pool.tensor_copy(expert_no[:, :], ints[:, E:2 * E]))
                pool.wait_ge(k["consts"], 1)
                st.settle()
                st.did(pool.iota(ints[:, 0:E], pattern=[[CAP, E]], base=0, channel_multiplier=0))
                st.settle()
                st.did(pool.tensor_copy(region[:, :], ints[:, 0:E]))
                st.did(pool.tensor_copy(next_row[:, :], ints[:, 0:E]))
                st.settle()
                st.did(pool.iota(ints[:, 0:1], pattern=[[0, 1]], base=0, channel_multiplier=1))
                st.settle()
                st.did(pool.tensor_copy(part_no[:, :], ints[:, 0:1]))
                st.settle()
                pool.wait_ge(k["pads_written"], 16)
                st.did(pool.iota(ints[:, 0:E], pattern=[[P, E]], base=PADS, channel_multiplier=1))
                st.settle()
                st.did(pool.tensor_copy(pad_rows[:, :, D:D + 1].bitcast(I32), ints[:, 0:E].unsqueeze(2)))
                st.settle()

            @block.tensor
            def _(pe):
                pe.wait_ge(k["small_loaded"], 12 * 16)
                pe.wait_ge(pool_s, 12)
                for c in range(4):
                    pe.transpose(chunk(bank[0], c), wst[:, c, :], ident[:, :])
                for n in range(4):
                    pe.transpose(chunk(bank[1], n), XN[:, 0, n, :], ident[:, :])
                for c in range(FC):
                    mm = pe.transpose(chunk(bank[2], c), wst[:, 4 + c, :], ident[:, :])
                mm.then_inc(k["prep_transposed"], 1)

            @block.vector
            def _(dve):
                st = Steps(dve, vec)
                dve.wait_ge(k["prep_transposed"], 1)
                st.did(dve.tensor_copy(SHT, bank[0][:, :]))
                st.did(dve.tensor_copy(WT4[:, :, :].rearrange("p n d -> p (n d)"), bank[1][:, :]))
                st.did(dve.tensor_copy(WOS[:, :, :].rearrange("p n d -> p (n d)"), bank[2][:, 0:F]))
                st.settle()
                st.did(dve.tensor_copy(SHH[:, :], SHT))
                dve.wait_ge(k["weights_loaded"], 48)
                st.did(dve.tensor_copy(WEH[:, :], stage))
                st.settle()
                st.did(dve.tensor_tensor(SHL[:, :], SHT, SHH[:, :].bitcast(F32), ALU.subtract))
                st.did(dve.tensor_tensor(WEL[:, :], stage, WEH[:, :].bitcast(F32), ALU.subtract))
                st.settle()
                vec_at.append(st.n)

        def xt_bank(done):
            return bank[7 if done else 0]

        def pe_route(pe, b, done):
            n = done + b.i
            pe.wait_ge(k["normed"], n + 1)
            if due(n):
                pe.wait_ge(k["xt_copied"], n)
            if done:
                pe.wait_ge(k["c_odd"], (b.i + 2) * 2 if not isinstance(b.i, int) else min(b.i + 2, NB) * 2)
            for j in range(BT):
                mm = pe.transpose(chunk(xt_bank(done), j), XN[:, b.buf, j, :], ident[:, :])
            mm.then_inc(k["xt_turned"], 1)

        def pe_score(pe, b, done):
            n = done + b.i
            pe.wait_ge(k["xt_copied"], n + 1)
            if due(n):
                pe.wait_ge(k["rank_read"], n)
            for j in range(BT):
                mm = pe.matmul(bank[1][:, j * E:(j + 1) * E], XT32[:, b.buf, j * P:(j + 1) * P], RT[:, :],
                               start=True, stop=True)
            mm.then_inc(k["scored"], 1)

        def pe_rank(pe, b, done):
            pe.wait_ge(k["picked"], done + b.i + 1)
            rk = bank[1][:, 0:BT * E]
            hot = HOTB[:, :, :].rearrange("p j e -> p (j e)")
            pe.matmul(rk, before[:, :], hot, start=True, stop=False)
            for s in range(1, BT):
                pe.matmul(rk[:, s * E:], ones[:, :], hot[:, 0:(BT - s) * E], start=False, stop=(s == BT - 1))
            tot = bank[1][:, BT * E:(BT + 1) * E]
            for j in range(BT):
                mm = pe.matmul(tot, ones[:, :], hot[:, j * E:(j + 1) * E], start=(j == 0), stop=(j == BT - 1))
            mm.then_inc(k["ranked"], 1)

        def act_copy_xt(act, b, done):
            n = done + b.i
            act.wait_ge(k["xt_turned"], n + 1)
            if due(n - 1):
                act.wait_ge(k["scored"], n - 1)
            if due(n - 1):
                act.wait_ge(k["xt_split"], n - 1)
            act.activation(XT32[:, b.buf, :], xt_bank(done)[:, :], ACT.Copy).then_inc(k["xt_copied"], 1)

        def act_gates(act, b, done):
            n = done + b.i
            act.wait_ge(k["topped"], n + 1)
            if due(n - 1):
                act.wait_ge(k["gate_done"], n - 1)
            act.activation(TNH[:, b.buf, :, :], TOP[:, b.buf, :, 0:TOPK], ACT.Tanh, scale=0.5)\
               .then_inc(k["tanh_done"], 1)

        def act_payload(act, b, done):
            n = done + b.i
            act.wait_ge(k["gate_done"], n + 1)
            if due(BT * TOPK * 16 * (done // 2 + b.uses)):
                act.wait_ge(scattered[b.buf], BT * TOPK * 16 * (done // 2 + b.uses))
            for j in range(BT):
                ins = act.activation(PAY[:, b.buf, 1, j, 0:D], XN[:, b.buf, j, :], ACT.Copy,
                                     scale=GATE[:, b.buf, j, 1:2])
            ins.then_inc(k["pay1"], 1)

        def dve_norm(dve, st, b, done):
            n = done + b.i
            if due(n - 1):
                dve.wait_ge(k["xt_turned"], n - 1)
            if due(n - 1):
                dve.wait_ge(k["pay1"], n - 1)
            for j in range(BT):
                t = BT * b.i + j
                mean = cut(MEAN, t, 1) if done == 0 else MV[:, 1, j, 0:1]
                rstd = cut(RSTD, t, 1) if done == 0 else RST[:, 1, j:j + 1]
                ins = dve.tensor_scalar(XN[:, b.buf, j:j + 1, :], tile_of(X, t), mean, rstd, ALU.subtract, ALU.mult)
            st.signals(ins, k["normed"], n + 1)

        def dve_split(dve, st, b, done):
            dve.wait_ge(k["xt_copied"], done + b.i + 1)
            if due(done + b.i - 1):
                dve.wait_ge(k["up1"], done + b.i - 1)
            hi, lo = XTH[:, b.buf, :], XTL[:, b.buf, :]
            st.did(dve.tensor_copy(hi, XT32[:, b.buf, :]))
            st.settle()
            st.signals(dve.tensor_tensor(lo, XT32[:, b.buf, :], hi.bitcast(F32), ALU.subtract), k["xt_split"], done + b.i + 1)

        def dve_keep(dve, st, b, done):
            dve.wait_ge(k["xt_copied"], done + b.i + 1)
            st.signals(dve.tensor_copy(cut(XTR, W * b.i, W), XT32[:, b.buf, :]), k["xt_split"], done + b.i + 1)

        def dve_split_kept(dve, st, b):
            if due(NB + b.i - 1):
                dve.wait_ge(k["up1"], NB + b.i - 1)
            hi, lo = XTH[:, b.buf, :], XTL[:, b.buf, :]
            st.did(dve.tensor_copy(hi, cut(XTR, W * b.i, W)))
            st.settle()
            st.signals(dve.tensor_tensor(lo, cut(XTR, W * b.i, W), hi.bitcast(F32), ALU.subtract), k["kept_split"], b.i + 1)

        def dve_top(dve, st, b, done):
            n = done + b.i
            dve.wait_ge(k["scored"], n + 1)
            st.did(dve.tensor_copy(SC[:, :, :].rearrange("p j e -> p (j e)"), bank[1][:, 0:BT * E]))
            st.settle()
            if due(n - 1):
                dve.wait_ge(k["tanh_done"], n - 1)
            carry(dve)
            for j in range(BT):
                ins = dve.max(TOP[:, b.buf, j, :], SC[:, j, :])
            st.signals(ins, k["topped"], n + 1)
            st.settle()
            carry(dve)
            for j in range(BT):
                st.did(dve.max_index(TOPI[:, j, :], TOP[:, b.buf, j, :], SC[:, j, :]))
            st.settle()
            st.did(dve.tensor_tensor(HOT[:, :, :, :],
                                     TOPI[:, :, 0:TOPK].unsqueeze(3).to_broadcast([P, BT, TOPK, E]),
                                     expert_no[:, :].unsqueeze(1).unsqueeze(1).to_broadcast([P, BT, TOPK, E]),
                                     ALU.is_equal))
            st.settle()
            st.signals(dve.tensor_tensor(HOTB[:, :, :], HOT[:, :, 0, :], HOT[:, :, 1, :], ALU.add), k["picked"], n + 1)

        def dve_payload(dve, st, b, done):
            n = done + b.i
            dve.wait_ge(k["tanh_done"], n + 1)
            if due(BT * TOPK * 16 * (done // 2 + b.uses)):
                dve.wait_ge(scattered[b.buf], BT * TOPK * 16 * (done // 2 + b.uses))
            st.signals(dve.tensor_scalar(GATE[:, b.buf, :, :], TNH[:, b.buf, :, :], 0.5, 0.5, ALU.mult, ALU.add), k["gate_done"], n + 1)
            where = dest[:, :, BT * b.i:BT * b.i + BT] if isinstance(b.i, int) else dest[:, :, ds(BT * b.i, BT)]
            st.did(dve.tensor_copy(PAY[:, b.buf, :, :, D:D + 1].bitcast(I32), where.unsqueeze(3)))
            st.settle()
            for j in range(BT):
                ins = dve.tensor_scalar(PAY[:, b.buf, 0, j, 0:D], XN[:, b.buf, j, :],
                                               GATE[:, b.buf, j, 0:1], None, ALU.mult)
            st.signals(ins, k["pay0"], n + 1)

        def dve_place(dve, st, b, done):
            dve.wait_ge(k["ranked"], done + b.i + 1)
            st.did(dve.tensor_tensor(RANK[:, :, :], bank[1][:, 0:BT * E].rearrange("p (j e) -> p j e", e=E),
                                     next_row[:, :].unsqueeze(1).to_broadcast([P, BT, E]), ALU.add))
            st.settle()
            st.signals(dve.tensor_tensor(next_row[:, :], bank[1][:, BT * E:(BT + 1) * E], next_row[:, :], ALU.add), k["rank_read"], done + b.i + 1)
            st.did(dve.tensor_tensor(PICK[:, :, :, :], HOT[:, :, :, :],
                                     RANK[:, :, :].unsqueeze(2).to_broadcast([P, BT, TOPK, E]), ALU.mult))
            st.settle()
            with nc.allow_low_precision(reason="row numbers: whole, below 2^24"):
                st.signals(dve.tensor_reduce(POS[:, b.buf, :, :], PICK[:, :, :, :], AXX, ALU.add), k["placed"], done + b.i + 1)

        def pool_scatter(pool, b, done):
            n = done + b.i
            pool.wait_ge(k["pay0"], n + 1)
            pool.wait_ge(k["pay1"], n + 1)
            pool.wait_ge(k["placed"], n + 1)
            pool_carry(pool, "carried_s", n)
            for j in range(BT):
                for c in range(TOPK):
                    pool.indirect_dma_start(pairs, bass.IndirectOffsetOnAxis(ap=POS[:, b.buf, j, c:c + 1], axis=0),
                                            PAY[:, b.buf, c, j, :], None).then_inc(scattered[b.buf], 16)

        def pe_shared_up(pe, b, done):
            n = done + b.i
            pe.wait_ge(k["xt_split" if done == 0 else "kept_split"], b.i + 1)
            hi, lo = XTH[:, b.buf, :], XTL[:, b.buf, :]
            for c in range(FC):
                if due(n):
                    pe.wait_ge(k[f"hid{c}"], n)
                for g in range(2):
                    ps = bank[2 + 2 * c + g]
                    w = slice(g * F + c * P, g * F + (c + 1) * P)
                    pe.matmul(ps[:, :], SHL[:, w], hi, start=True, stop=False)
                    pe.matmul(ps[:, :], SHH[:, w], lo, start=False, stop=False)
                    mm = pe.matmul(ps[:, :], SHH[:, w], hi, start=False, stop=True)
                mm.then_inc(k[f"up{c}"], 1)

        def act_shared(act, b, done):
            n = done + b.i
            for c in range(FC):
                act.wait_ge(k[f"up{c}"], n + 1)
                if due(n):
                    act.wait_ge(k[f"hid{c}"], n)
                act.activation(SSG[:, c, :], bank[2 + 2 * c][:, :], ACT.Silu).then_inc(k[f"silu{c}"], 1)

        def dve_shared_mul(dve, st, b, done):
            n = done + b.i
            if due(n):
                dve.wait_ge(k["down"], n)
            for c in range(FC):
                dve.wait_ge(k[f"silu{c}"], n + 1)
                st.signals(dve.tensor_tensor(SHH_T[:, c, :], bank[3 + 2 * c][:, :], SSG[:, c, :], ALU.mult), k[f"hid{c}"], n + 1)

        def pe_shared_down(pe, b, done):
            n = done + b.i
            pe.wait_ge(k["hid0"], n + 1)
            pe.wait_ge(k["hid1"], n + 1)
            if due(n):
                pe.wait_ge(k["shared_added"], n)
            for j in range(BT):
                for c in range(FC):
                    mm = pe.matmul(chunk(bank[6], j), SHH_T[:, c, j * P:(j + 1) * P], WOS[:, c, :],
                                   start=(c == 0), stop=(c == FC - 1))
            mm.then_inc(k["down"], 1)

        def dve_shared_add(dve, st, b, done):
            dve.wait_ge(k["down"], done + b.i + 1)
            st.signals(dve.scalar_tensor_tensor(out=x_block(b), in0=bank[6][:, :].rearrange("p (j d) -> p j d", d=D),
                                            scalar=0.5, in1=x_block(b), op0=ALU.mult, op1=ALU.add), k["shared_added"], done + b.i + 1)

        A_STATS = 2 * BT * 2
        with nc.Block() as block:
            @block.sync
            def _(sp):
                def load(at):
                    b = at(0)
                    if due(16 * b.uses):
                        sp.wait_ge(x_loaded[b.buf], 16 * b.uses)
                    sp.dma_start(x_block(b), x_t[:, BT * b.i:BT * b.i + BT, :] if isinstance(b.i, int)
                                 else x_t[:, ds(BT * b.i, BT), :]).then_inc(x_loaded[b.buf], 16)
                rolled(sp, NB, 0, 0, load)

            @block.vector
            def _(dve):
                st = Steps(dve, vec, vec_at[0])
                def stats(at):
                    b = at(0)
                    dve.wait_ge(x_loaded[b.buf], 16 * (b.uses + 1))
                    carry(dve)
                    for j in range(BT):
                        st.did(dve.bn_stats(ST[:, b.buf, j, :], tile_of(X, BT * b.i + j).rearrange("p a d -> p (a d)")))
                    st.settle()
                    carry(dve)
                    for j in range(BT):
                        ins = dve.bn_aggr(MV[:, 0, j, :], ST[:, b.buf, j, :])
                    st.did(ins)
                    st.settle()
                    for c, all_of in enumerate((MEAN, VAR)):
                        ins = dve.tensor_copy(cols(all_of, b), MV[:, 0, :, c])
                    st.signals(ins, k["stats_done"], b.i + 1)
                    st.settle()
                rolled(dve, NB, 0, 0, stats, st, 2 * (BT + 1))
                dve.wait_ge(k["std_done"], 1)
                st.did(dve.reciprocal(RSTD[:, :], STD[:, :]))
                st.settle()

                def body(at):
                    new, b = at(1), at(0)
                    if new.live:
                        dve_norm(dve, st, new, 0)
                    if b.live:
                        dve_shared_mul(dve, st, b, 0)
                    if new.live:
                        dve_split(dve, st, new, 0)
                        dve_top(dve, st, new, 0)
                    if b.live:
                        dve_shared_add(dve, st, b, 0)
                    if new.live:
                        dve_payload(dve, st, new, 0)
                        dve_place(dve, st, new, 0)
                rolled(dve, NB, 1, 0, body, st, 2 * (1 + 6 + 1 + 2))
                vec_at[0] = st.base + st.n

            @block.scalar
            def _(act):
                act.wait_ge(k["stats_done"], NB)
                act.activation(STD[:, :], VAR[:, :], ACT.Sqrt, bias=eps_c[:, :]).then_inc(k["std_done"], 1)

                def body(at):
                    new, b = at(1), at(0)
                    if new.live:
                        act_copy_xt(act, new, 0)
                    if b.live:
                        act_shared(act, b, 0)
                    if new.live:
                        act_gates(act, new, 0)
                        act_payload(act, new, 0)
                rolled(act, NB, 1, 0, body)

            @block.tensor
            def _(pe):
                def body(at):
                    new, b = at(1), at(0)
                    if new.live:
                        pe_route(pe, new, 0)
                    if b.live:
                        pe_shared_up(pe, b, 0)
                    if new.live:
                        pe_score(pe, new, 0)
                    if b.live:
                        pe_shared_down(pe, b, 0)
                    if new.live:
                        pe_rank(pe, new, 0)
                rolled(pe, NB, 1, 0, body)

            @block.gpsimd
            def _(pool):
                rolled(pool, NB, 0, 0, lambda at: pool_scatter(pool, at(0), 0))
                for s in scattered:
                    pool.wait_ge(s, BT * TOPK * 16 * NB // 2)

        def experts(done):
            first = done == 0
            ffn = 0 if first else 1
            with nc.Block() as block:
                @block.vector
                def _(dve):
                    st = Steps(dve, vec, vec_at[0])
                    st.did(dve.tensor_scalar(pad_at[:, :], next_row[:, :], part_no[:, :], None, ALU.add))
                    cnt, tiles, ends = tcnt[:, 0, :], tcnt[:, 1, :], tcnt[:, 2, :]
                    st.did(dve.tensor_tensor(cnt, next_row[0:1, :], region[0:1, :], ALU.subtract))
                    st.settle()
                    st.did(dve.tensor_scalar(tcnt_i[:, 0, :], cnt, float(P - 1), None, ALU.add))
                    st.settle()
                    st.did(dve.tensor_scalar(tcnt_i[:, 1, :], tcnt_i[:, 0, :], 7, None, ALU.arith_shift_right))
                    st.settle()
                    st.did(dve.tensor_copy(tiles, tcnt_i[:, 1, :]))
                    st.settle()
                    st.did(dve.tensor_tensor(tee[:, :, :], upto[:, :, :], tiles.unsqueeze(1).to_broadcast([1, E, E]), ALU.mult))
                    st.settle()
                    st.did(dve.tensor_reduce(ends, tee[:, :, :], AXX, ALU.add))
                    st.settle()
                    tbl = big[0:1, 0, :, :].rearrange("p a w -> p (a w)")[:, 0:NT * E].rearrange("p (t e) -> p t e", e=E)
                    st.did(dve.tensor_tensor(tbl, tile_no[:, :].unsqueeze(2).to_broadcast([1, NT, E]),
                                             ends.unsqueeze(1).to_broadcast([1, NT, E]), ALU.is_ge))
                    st.settle()
                    ex, gone, row = tot_t[:, 0, :], tot_t[:, 1, :], tot_t[:, 2, :]
                    st.did(dve.tensor_reduce(ex, tbl, AXX, ALU.add))
                    st.settle()
                    st.did(dve.tensor_tensor(tbl, tbl, tiles.unsqueeze(1).to_broadcast([1, NT, E]), ALU.mult))
                    st.settle()
                    st.did(dve.tensor_reduce(gone, tbl, AXX, ALU.add))
                    st.did(dve.tensor_scalar(expert_of[:, :], ex, float(E - 1), None, ALU.min))
                    st.settle()
                    st.did(dve.tensor_tensor(row, tile_no[:, :], gone, ALU.subtract))
                    st.did(dve.tensor_scalar(ex, ex, float(CAP), None, ALU.mult))
                    st.settle()
                    st.did(dve.scalar_tensor_tensor(out=row_of[:, :], in0=row, scalar=float(P), in1=ex,
                                                    op0=ALU.mult, op1=ALU.add))
                    st.signals(dve.tensor_copy(next_row[:, :], region[:, :]), k["table_done"], ffn + 1)
                    st.settle()

                    def body(at):
                        nx, t, od = at(2), at(0), at(-2)
                        if t.live:
                            dve.wait_ge(k["e_silu"], done + t.i + 1)
                            if due(done + t.i - 1):
                                dve.wait_ge(k["e_turned"], done + t.i - 1)
                            st.signals(dve.tensor_tensor(H[:, t.buf % 2, :], bank[2 + t.buf % 2][:, F:2 * F],
                                                     SG[:, t.buf % 2, :], ALU.mult), k["e_hid"], done + t.i + 1)
                        if od.live:
                            dve.wait_ge(k["e_down"], done + od.i + 1)
                            if due(16 * (done // SLOTS + od.uses)):
                                dve.wait_ge(y_sent[od.buf], 16 * (done // SLOTS + od.uses))
                            st.signals(dve.tensor_scalar(YO[:, od.buf, :], bank[6 + od.buf % 2][:, 0:D], 0.5, None,
                                                     ALU.mult), k["e_out"], done + od.i + 1)
                        if nx.live:
                            dve.wait_ge(k["xs_high"], done + nx.i + 1)
                            if due(done + nx.i - 1):
                                dve.wait_ge(k["e_up"], done + nx.i - 1)
                            st.signals(dve.tensor_tensor(XSL[:, nx.buf % 2, :], bank[nx.buf % 2][:, 0:P],
                                                     XSH[:, nx.buf % 2, :].bitcast(F32), ALU.subtract), k["xs_low"], done + nx.i + 1)
                    rolled(dve, NT, 2, 2, body, st, 0, n=SLOTS, peel=SLOTS)
                    vec_at[0] = st.base + st.n

                @block.gpsimd
                def _(pool):
                    pool.wait_ge(k["table_done"], ffn + 1)
                    for e in range(E):
                        pool.indirect_dma_start(pairs, bass.IndirectOffsetOnAxis(ap=pad_at[:, e:e + 1], axis=0),
                                                pad_rows[:, e, :], None).then_inc(k["stored_y"], 16)

                    def send(at):
                        t = at(0)
                        pool.wait_ge(k["e_out"], done + t.i + 1)
                        pool_carry(pool, "carried_y", done + t.i)
                        pool.indirect_dma_start(
                            results, bass.IndirectOffsetOnAxis(ap=XS[:, t.buf, D:D + 1].bitcast(U32), axis=0),
                            YO[:, t.buf, :], None).then_inc(y_sent[t.buf], 16)
                    rolled(pool, NT, 0, 0, send, n=SLOTS)
                    for s in y_sent:
                        pool.wait_ge(s, 16 * (done + NT) // SLOTS)

                @block.sync
                def _(sp):
                    sp.wait_ge(k["table_done"], ffn + 1)
                    sp.wait_ge(k["stored_y"], 16 * E * (ffn + 1))
                    rows = [sp.alloc_register(f"row{ffn}_{i}") for i in range(SLOTS)]
                    def load(r):
                        sp.reg_load(rows, row_of[0:1, ds(r * SLOTS, SLOTS)])
                        for u in range(SLOTS):
                            row = sp.snap(rows[u], min_val=0, max_val=E * CAP + (DUMMY - 1) * P)
                            if due((r + done // SLOTS) * 16):
                                sp.wait_ge(y_sent[u], (r + done // SLOTS) * 16)
                            sp.dma_start(XS[:, u, :], pairs[ds(row, P), :]).then_inc(xs_loaded[u], 16)
                    load(0)
                    with sp.Fori(1, NT // SLOTS) as r:
                        load(r)

                @block.scalar
                def _(act):
                    def body(at):
                        nx, t, ld = at(2), at(0), at(-1)
                        if t.live:
                            act.wait_ge(k["e_up"], done + t.i + 1)
                            if due(done + t.i - 1):
                                act.wait_ge(k["e_hid"], done + t.i - 1)
                            act.activation(SG[:, t.buf % 2, :], bank[2 + t.buf % 2][:, 0:F], ACT.Silu)\
                               .then_inc(k["e_silu"], 1)
                        if ld.live:
                            act.wait_ge(k["e_turned"], done + ld.i + 1)
                            if due(done + ld.i - 1):
                                act.wait_ge(k["e_down"], done + ld.i - 1)
                            act.activation(HT[:, ld.buf % 2, :], bank[4 + ld.buf % 2][:, 0:F], ACT.Copy)\
                               .then_inc(k["e_copied"], 1)
                        if nx.live:
                            act.wait_ge(k["xs_turned"], done + nx.i + 1)
                            if due(done + nx.i - 1):
                                act.wait_ge(k["e_up"], done + nx.i - 1)
                            act.activation(XSH[:, nx.buf % 2, :], bank[nx.buf % 2][:, 0:P], ACT.Copy)\
                               .then_inc(k["xs_high"], 1)
                    rolled(act, NT, 2, 1, body, n=SLOTS)

                @block.tensor
                def _(pe):
                    pe.wait_ge(k["table_done"], ffn + 1)
                    regs = [pe.alloc_register(f"expert{ffn}_{i}") for i in range(SLOTS + 2)]

                    def expert(reg):
                        return pe.snap(reg, min_val=0, max_val=E - 1)

                    def body(nx, t, ld, od, up_reg, down_reg):
                        if t.live:
                            e = expert(up_reg)
                            ps = bank[2 + t.buf % 2][:, :]
                            hi, lo = XSH[:, t.buf % 2, :], XSL[:, t.buf % 2, :]
                            pe.wait_ge(k["xs_low"], done + t.i + 1)
                            if due(done + t.i - 1):
                                pe.wait_ge(k["e_hid"], done + t.i - 1)
                            pe.matmul(ps, lo, WEH[:, ds(e * 2 * F, 2 * F)], start=True, stop=False)
                            pe.matmul(ps, hi, WEL[:, ds(e * 2 * F, 2 * F)], start=False, stop=False)
                            pe.matmul(ps, hi, WEH[:, ds(e * 2 * F, 2 * F)], start=False, stop=True)\
                              .then_inc(k["e_up"], 1)
                        if od.live:
                            e = expert(down_reg)
                            pe.wait_ge(k["e_copied"], done + od.i + 1)
                            if due(done + od.i - 1):
                                pe.wait_ge(k["e_out"], done + od.i - 1)
                            for c in range(FC):
                                mm = pe.matmul(bank[6 + od.buf % 2][:, 0:D], HT[:, od.buf % 2, c * P:(c + 1) * P],
                                               WOE[:, ds(e * FC * D + c * D, D)], start=(c == 0), stop=(c == FC - 1))
                            mm.then_inc(k["e_down"], 1)
                        if ld.live:
                            pe.wait_ge(k["e_hid"], done + ld.i + 1)
                            if due(done + ld.i - 1):
                                pe.wait_ge(k["e_copied"], done + ld.i - 1)
                            for c in range(FC):
                                mm = pe.transpose(chunk(bank[4 + ld.buf % 2], c), H[:, ld.buf % 2, c * P:(c + 1) * P],
                                                  ident[:, :])
                            mm.then_inc(k["e_turned"], 1)
                        if nx.live:
                            pe.wait_ge(xs_loaded[nx.buf], 16 * (done // SLOTS + nx.uses + 1))
                            if due(done + nx.i - 1):
                                pe.wait_ge(k["xs_low"], done + nx.i - 1)
                            pe.transpose(bank[nx.buf % 2][:, 0:P], XS[:, nx.buf, 0:D], ident[:, :])\
                              .then_inc(k["xs_turned"], 1)

                    def some(lo, hi):
                        of = range(max(lo - 2, 0), min(hi, NT))
                        pe.reg_load(regs[:len(of)], expert_of[0:1, of[0]:of[-1] + 1])
                        for i in range(lo, hi):
                            def at(d):
                                return At(i + d, (i + d) % SLOTS, (i + d) // SLOTS, NT)
                            body(at(2), at(0), at(-1), at(-2), regs[of.index(i)] if i in of else None,
                                 regs[of.index(i - 2)] if i - 2 in of else None)

                    turns = (NT - 6) // SLOTS
                    some(-2, 4)
                    with pe.Fori(0, turns) as r:
                        pe.reg_load(regs, expert_of[0:1, ds(r * SLOTS + 2, SLOTS + 2)])
                        for u in range(SLOTS):
                            def at(d):
                                return At(r * SLOTS + (4 + u + d), (4 + u + d) % SLOTS, r + (4 + u + d) // SLOTS, NT)
                            body(at(2), at(0), at(-1), at(-2), regs[u + 2], regs[u])
                    some(4 + turns * SLOTS, NT + 2)

        experts(0)

        def load_y(sp, b, done):
            if due(done + b.i - 1):
                sp.wait_ge(k["combined"], done + b.i - 1)
            src = results_t[:, :, BT * b.i:BT * b.i + BT, :] if isinstance(b.i, int) else results_t[:, :, ds(BT * b.i, BT), :]
            for c in range(TOPK):
                sp.dma_start(Y2[:, b.buf, c, :, :], src[:, c, :, :]).then_inc(y_loaded[b.buf], 8 * 2)

        def up_to(b, more):
            return b.i + more if not isinstance(b.i, int) else min(b.i + more, NB)

        with nc.Block() as block:
            @block.sync
            def _(sp):
                rolled(sp, NB, 0, 0, lambda at: load_y(sp, at(0), 0))

            @block.vector
            def _(dve):
                st = Steps(dve, vec, vec_at[0])

                def maximum(b, a):
                    dve.wait_ge(k["s_made"], BT * b.i + (a + 1))
                    if a == 0 and due(BT * b.i - BT):
                        dve.wait_ge(k["probs_ready"], BT * b.i - BT)
                    st.signals(dve.tensor_reduce(NM[:, b.buf, a, :],
                                                 bank[4 + a % 2][:, :].rearrange("p (g c) -> p g c", c=P),
                                                 AXX, ALU.max, negate=True), k["m_ready"], BT * b.i + (a + 1))

                def normalise(new):
                    if due(new.i):
                        dve.wait_ge(k["a_turned"], new.i)
                    for j in range(BT):
                        ins = dve.tensor_scalar(AN[:, j:j + 1, :], tile_of(X, BT * new.i + j),
                                                MV[:, 0, j, 0:1], RST[:, 0, j:j + 1],
                                                ALU.subtract, ALU.mult)
                    st.signals(ins, k["a_normed"], new.i + 1)

                def add_result(b, c, after):
                    dve.wait_ge(*after)
                    ins = dve.tensor_tensor(x_block(b), x_block(b), Y2[:, b.buf, c, :, :], ALU.add)
                    if c == TOPK - 1:
                        st.signals(ins, k["combined"], b.i + 1)
                    else:
                        st.did(ins)
                    return st.mark()

                def moments(b, which, after):
                    dve.wait_ge(*after)
                    carry(dve, 1 + which)
                    for j in range(BT):
                        st.did(dve.bn_stats(ST[:, which, j, :],
                                            tile_of(X, BT * b.i + j).rearrange("p a d -> p (a d)")))
                    return st.mark()

                def mean_var(b, which, after, done_sem):
                    dve.wait_ge(*after)
                    carry(dve, 3 + which)
                    for j in range(BT):
                        ins = dve.bn_aggr(MV[:, which, j, :], ST[:, which, j, :])
                    st.signals(ins, done_sem, b.i + 1)

                def update(c):
                    dve.wait_ge(k["proj_made"], c.i + 1)
                    st.signals(dve.tensor_tensor(x_block(c), bank[3][:, :].rearrange("p (j d) -> p j d", d=D),
                                                 x_block(c), ALU.add), k["updated"], c.i + 1)
                    return st.mark()

                def weight(b, n, after):
                    dve.wait_ge(*after)
                    sm = SUM[:, b.buf, :, :]
                    if n == 0:
                        ins = dve.reciprocal(R1[:, :, :], sm)
                    elif n == 1:
                        ins = dve.tensor_tensor(R2[:, :, :], R1[:, :, :], sm, ALU.mult)
                    elif n == 2:
                        ins = dve.tensor_reduce(R3[:, :, :], R2[:, :, :].unsqueeze(2), AXX, ALU.add)
                    elif n == 3:
                        ins = dve.tensor_scalar(R3[:, :, :], R3[:, :, :], 1e-6, None, ALU.add)
                    elif n == 4:
                        ins = dve.reciprocal(R4[:, :, :], R3[:, :, :])
                    else:
                        ins = dve.tensor_tensor(R2[:, :, :], R1[:, :, :], R4[:, :, :].to_broadcast([P, BT, G]),
                                                ALU.mult)
                    st.did(ins)
                    return st.mark()

                def scale(b, a, after):
                    if a == 0:
                        dve.wait_ge(*after)
                    e3 = big[:, b.buf, a, :].rearrange("p (g c) -> p g c", c=P)
                    st.signals(dve.tensor_tensor(e3, e3, R2[:, a, :].unsqueeze(2).to_broadcast([P, G, P]),
                                                 ALU.mult), k["scaled"], BT * b.i + (a + 1))

                def body(at):
                    ahead, new, b, c, old, out = at(2), at(1), at(0), at(-1), at(-2), at(-3)
                    if b.live:
                        maximum(b, 0)
                        maximum(b, 1)
                    if new.live:
                        dve.wait_ge(k["a_std"], new.i + 1)
                        st.did(dve.reciprocal(RST[:, 0, :], SD[:, 0, :]))
                    if old.live:
                        dve.wait_ge(k["r_std"], old.i + 1)
                        st.did(dve.reciprocal(RST[:, 1, :], SD[:, 1, :]))
                    st.settle()
                    if new.live:
                        normalise(new)
                    if b.live:
                        maximum(b, 2)
                    if old.live:
                        dve_norm(dve, st, old, NB)
                    if ahead.live:
                        added = add_result(ahead, 0, (y_loaded[ahead.buf], 32 * (ahead.uses + 1)))
                    if out.live:
                        dve_top(dve, st, out, NB)
                    if b.live:
                        maximum(b, 3)
                    if out.live:
                        dve_payload(dve, st, out, NB)
                        dve_place(dve, st, out, NB)
                    if ahead.live:
                        added = add_result(ahead, 1, added)
                    if c.live:
                        updated = update(c)
                    if b.live:
                        r1 = weight(b, 0, (k["probs_ready"], BT * (b.i + 1)))
                    if ahead.live:
                        seen = moments(ahead, 0, added)
                    if b.live:
                        r2 = weight(b, 1, r1)
                    if c.live:
                        seen_c = moments(c, 1, updated)
                    if b.live:
                        r3 = weight(b, 2, r2)
                    if ahead.live:
                        mean_var(ahead, 0, seen, k["a_stats"])
                    if b.live:
                        r3 = weight(b, 3, r3)
                    if c.live:
                        mean_var(c, 1, seen_c, k["r_stats"])
                    if b.live:
                        r4 = weight(b, 4, r3)
                    if old.live:
                        dve_keep(dve, st, old, NB)
                    if b.live:
                        r5 = weight(b, 5, r4)
                        for a in range(BT):
                            scale(b, a, r5)
                rolled(dve, NB, 2, 3, body, st, 2 * 26)
                vec_at[0] = st.base + st.n

            @block.scalar
            def _(act):
                def exps(b, a):
                    act.wait_ge(k["m_ready"], BT * b.i + (a + 1))
                    if a == 0 and due(2 * (b.i - 1)):
                        act.wait_ge(k["t_odd"], 2 * (b.i - 1))
                    for g in range(G):
                        ins = act.activation(big[:, b.buf, a, g * P:(g + 1) * P], chunk(bank[4 + a % 2], g),
                                             ACT.Exp, bias=NM[:, b.buf, a, g:g + 1],
                                             accum_out=SUM[:, b.buf, a, g:g + 1])
                    ins.then_inc(k["probs_ready"], 1)

                def copy_turned(c, g):
                    h = g // 2
                    if g % 2 == 0:
                        act.wait_ge(k["t_even"], 2 * c.i + (h + 1))
                        if due(2 * (2 * c.i + h) - 1):
                            act.wait_ge(k["av_made"], 2 * (2 * c.i + h) - 1)
                        act.activation(PT[:, 0, :], bank[6][:, :], ACT.Copy).then_inc(k["c_even"], 1)
                    else:
                        act.wait_ge(k["t_odd"], 2 * c.i + (h + 1))
                        if due(2 * (2 * c.i + h)):
                            act.wait_ge(k["av_made"], 2 * (2 * c.i + h))
                        act.activation(PT[:, 1, :], bank[7][:, :], ACT.Copy).then_inc(k["c_odd"], 1)

                def body(at):
                    new, b, c, old, out = at(1), at(0), at(-1), at(-2), at(-3)
                    if new.live:
                        act.wait_ge(k["a_stats"], new.i + 1)
                        act.activation(SD[:, 0, :], MV[:, 0, :, 1], ACT.Sqrt, bias=eps_c[:, :])\
                           .then_inc(k["a_std"], 1)
                    if old.live:
                        act.wait_ge(k["r_stats"], old.i + 1)
                        act.activation(SD[:, 1, :], MV[:, 1, :, 1], ACT.Sqrt, bias=eps_c[:, :])\
                           .then_inc(k["r_std"], 1)
                    for a in range(BT):
                        if b.live:
                            exps(b, a)
                        if c.live:
                            copy_turned(c, a)
                    if out.live:
                        act_gates(act, out, NB)
                    if new.live:
                        act.wait_ge(k["a_turned"], new.i + 1)
                        if due(new.i):
                            act.wait_ge(k["k_made"], new.i)
                        act.activation(AXT, bank[0][:, :], ACT.Copy).then_inc(k["a_copied"], 1)
                    if c.live:
                        act.wait_ge(k["av_made"], 4 * (c.i + 1))
                        if due(c.i):
                            act.wait_ge(k["proj_made"], c.i)
                        act.activation(OT, bank[2][:, :], ACT.Copy).then_inc(k["ot_ready"], 1)
                    if out.live:
                        act_payload(act, out, NB)
                    if new.live:
                        act.wait_ge(k["q_made"], new.i + 1)
                        if due(BT * new.i):
                            act.wait_ge(k["s_made"], BT * new.i)
                        act.activation(QT, bank[2][:, :], ACT.Identity, bias=bq_s[:, :], scale=SCALE)\
                           .then_inc(k["q_ready"], 1)
                    if old.live:
                        act_copy_xt(act, old, NB)
                    if new.live:
                        act.wait_ge(k["v_made"], new.i + 1)
                        if due(4 * (new.i - 1)):
                            act.wait_ge(k["av_made"], 4 * (new.i - 1))
                        act.activation(V[:, new.buf, :, :].rearrange("p g d -> p (g d)"), bank[6][:, :], ACT.Copy)\
                           .then_inc(k["v_ready"], 1)
                        act.wait_ge(k["k_made"], new.i + 1)
                        if due(BT * new.i):
                            act.wait_ge(k["s_made"], BT * new.i)
                        act.activation(KT, bank[3][:, :], ACT.Identity, bias=bk_s[:, :]).then_inc(k["k_ready"], 1)
                rolled(act, NB, 1, 3, body)

            @block.tensor
            def _(pe):
                def score(b, a):
                    if a == 0:
                        pe.wait_ge(k["q_ready"], b.i + 1)
                        pe.wait_ge(k["k_ready"], b.i + 1)
                    if due(BT * b.i + (a - 1)):
                        pe.wait_ge(k["probs_ready"], BT * b.i + (a - 1))
                    pe.matmul(bank[4 + a % 2][:, :], QT[:, a * P:(a + 1) * P], KT,
                              start=True, stop=True).then_inc(k["s_made"], 1)

                def turn(c, g):
                    name = ("even", "odd")[g % 2]
                    if g == 0:
                        pe.wait_ge(k["scaled"], BT * (c.i + 1))
                        pe.wait_ge(k["v_ready"], up_to(c, 2))
                    if g == 1 and due(c.i - 1):
                        pe.wait_ge(k["xt_copied"], NB + c.i - 1)
                    if due(2 * c.i + g // 2):
                        pe.wait_ge(k["c_" + name], 2 * c.i + g // 2)
                    for a in range(BT):
                        mm = pe.transpose(chunk(bank[6 + g % 2], a), big[:, c.buf, a, g * P:(g + 1) * P],
                                          ident[:, :])
                    mm.then_inc(k["t_" + name], 1)

                def times_values(c, g):
                    name = ("even", "odd")[g % 2]
                    pe.wait_ge(k["c_" + name], 2 * c.i + (g // 2 + 1))
                    if g == 0:
                        pe.wait_ge(k["q_ready"], up_to(c, 2))
                    pe.matmul(bank[2][:, :], V[:, c.buf, g, :], PT[:, g % 2, :], start=(g == 0),
                              stop=(g == G - 1)).then_inc(k["av_made"], 1)

                def body(at):
                    new, b, c, old, out = at(1), at(0), at(-1), at(-2), at(-3)
                    if b.live:
                        score(b, 0)
                        score(b, 1)
                    if c.live:
                        turn(c, 0)
                        turn(c, 1)
                    if b.live:
                        score(b, 2)
                    if c.live:
                        times_values(c, 0)
                        turn(c, 2)
                    if new.live:
                        pe.wait_ge(k["a_normed"], new.i + 1)
                        if due(new.i):
                            pe.wait_ge(k["a_copied"], new.i)
                        for j in range(BT):
                            mm = pe.transpose(chunk(bank[0], j), AN[:, j, :], ident[:, :])
                        mm.then_inc(k["a_turned"], 1)
                    if b.live:
                        score(b, 3)
                    if c.live:
                        times_values(c, 1)
                        turn(c, 3)
                        times_values(c, 2)
                    if out.live:
                        pe_rank(pe, out, NB)
                    if c.live:
                        times_values(c, 3)
                    if old.live:
                        pe_route(pe, old, NB)
                    if c.live:
                        pe.wait_ge(k["ot_ready"], c.i + 1)
                        pe.wait_ge(k["k_ready"], up_to(c, 2))
                        for j in range(BT):
                            pe.matmul(chunk(bank[3], j), OT[:, j * P:(j + 1) * P], WT4[:, 3, :], start=True, stop=False)
                            mm = pe.matmul(chunk(bank[3], j), one_row[:, :], bias_row[:, 1, :], start=False, stop=True)
                        mm.then_inc(k["proj_made"], 1)
                    if new.live:
                        pe.wait_ge(k["a_copied"], new.i + 1)
                        if due(new.i - 1):
                            pe.wait_ge(k["ot_ready"], new.i - 1)
                        pe.matmul(bank[2][:, :], WT4[:, 0, :], AXT, start=True, stop=True)\
                          .then_inc(k["q_made"], 1)
                        if due(2 * (new.i - 1)):
                            pe.wait_ge(k["c_even"], 2 * (new.i - 1))
                        for j in range(BT):
                            pe.matmul(chunk(bank[6], j), AXT[:, j * P:(j + 1) * P], WT4[:, 2, :],
                                      start=True, stop=False)
                            mm = pe.matmul(chunk(bank[6], j), one_row[:, :], bias_row[:, 0, :], start=False, stop=True)
                        mm.then_inc(k["v_made"], 1)
                        if due(new.i - 1):
                            pe.wait_ge(k["updated"], new.i - 1)
                        pe.matmul(bank[3][:, :], WT4[:, 1, :], AXT, start=True, stop=True)\
                          .then_inc(k["k_made"], 1)
                    if old.live:
                        pe_score(pe, old, NB)
                rolled(pe, NB, 1, 3, body)

            @block.gpsimd
            def _(pool):
                rolled(pool, NB, 0, 0, lambda at: pool_scatter(pool, at(0), NB))
                for s in scattered:
                    pool.wait_ge(s, BT * TOPK * 16 * NB)

        experts(NT)

        with nc.Block() as block:
            @block.sync
            def _(sp):
                rolled(sp, NB, 0, 0, lambda at: load_y(sp, at(0), NB))

            @block.tensor
            def _(pe):
                def body(at):
                    new, b = at(1), at(0)
                    if new.live:
                        pe_shared_up(pe, new, NB)
                    if b.live:
                        pe_shared_down(pe, b, NB)
                rolled(pe, NB, 1, 0, body)

            @block.scalar
            def _(act):
                def body(at):
                    new, b = at(1), at(0)
                    if new.live:
                        act_shared(act, new, NB)
                    if b.live:
                        act.wait_ge(k["combined"], NB + b.i + 1)
                        act.dma_start(out_t[:, BT * b.i:BT * b.i + BT, :] if isinstance(b.i, int)
                                      else out_t[:, ds(BT * b.i, BT), :], x_block(b)).then_inc(stored[b.buf], 16)
                        act.wait_ge(stored[b.buf], 16 * (b.uses + 1))
                rolled(act, NB, 1, 0, body)

            @block.vector
            def _(dve):
                st = Steps(dve, vec, vec_at[0])
                def body(at):
                    new, b, nxt = at(1), at(0), at(2)
                    if nxt.live:
                        dve_split_kept(dve, st, nxt)
                    if new.live:
                        dve_shared_mul(dve, st, new, NB)
                    if b.live:
                        dve_shared_add(dve, st, b, NB)
                        dve.wait_ge(y_loaded[b.buf], 32 * (NB // 2 + b.uses + 1))
                        st.settle()
                        st.did(dve.tensor_tensor(x_block(b), x_block(b), Y2[:, b.buf, 0, :, :], ALU.add))
                        st.settle()
                        st.signals(dve.tensor_tensor(x_block(b), x_block(b), Y2[:, b.buf, 1, :, :], ALU.add), k["combined"], NB + b.i + 1)
                rolled(dve, NB, 2, 0, body, st, 2 * 2)


_INS = ["L0_attn_batch", "L0_attn_Wq", "L0_attn_bq", "L0_attn_Wk", "L0_attn_bk", "L0_attn_Wv", "L0_attn_bv",
        "L0_attn_Wo", "L0_attn_bo", "L0_ffn_router_DE", "L0_ffn_w_in_shared_FD", "L0_ffn_w_out_shared_DF",
        "L0_ffn_w_swiglu_FD", "L0_ffn_w_in_eDF", "L0_ffn_w_swiglu_eDF", "L0_ffn_w_out_eFD"]


def kernel(**inputs):
    import numpy as np
    import concourse.bacc as bacc
    from concourse.bass_utils import run_bass_kernel_spmd as run

    nc = bacc.Bacc("TRN2", target_bir_lowering=False, num_devices=1)
    arrays, args = {}, []
    for name in _INS:
        a = np.ascontiguousarray(inputs[name])
        arrays[name] = a
        args.append(nc.dram_tensor(name, a.shape, mybir.dt.from_np(a.dtype), kind="ExternalInput").ap())
    shape = arrays["L0_attn_batch"].shape
    args.append(nc.dram_tensor("out", shape, F32, kind="ExternalOutput").ap())
    macaron(nc, *args)
    r = run(nc, [arrays], core_ids=[0])
    return r.results[0]["out"]
```

```python
from contextlib import ExitStack

import concourse.bass as bass
from concourse import mybir

F32 = mybir.dt.float32
F32R = mybir.dt.float32r
BF16 = mybir.dt.bfloat16
I32 = mybir.dt.int32
U32 = mybir.dt.uint32
ACT = mybir.ActivationFunctionType
ALU = mybir.AluOpType
AXX = mybir.AxisListType.X

P = 128
BT = 4
TOPK = 2
EPS = 1e-5
ds = bass.ds


class Steps:

    def __init__(self, eng, sem, n=0):
        self.eng, self.sem, self.base, self.n, self.last = eng, sem, 0, n, None

    def did(self, ins):
        ins.then_inc(self.sem, 1)
        self.n += 1
        self.last = None
        return ins

    def signals(self, ins, sem, count):
        ins.then_inc(sem, 1)
        self.last = sem, count

    def mark(self):
        return self.last or (self.sem, self.base + self.n)

    def settle(self):
        self.eng.wait_ge(*self.mark())

    def enter(self, turn, per_turn):
        self.before = self.base + self.n
        self.base, self.n = self.before + turn * per_turn, 0

    def leave(self, turns, per_turn):
        assert self.n == per_turn, f"steps in a turn of the loop: {self.n}, not {per_turn}"
        self.base, self.n = self.before + turns * per_turn, 0


class At:

    def __init__(self, i, buf, uses, total):
        self.i, self.buf, self.uses = i, buf, uses
        self.live = not isinstance(i, int) or 0 <= i < total


def rolled(eng, total, ahead, behind, body, steps=None, per_turn=0, n=2, peel=2):
    first = -(-(behind + peel) // n) * n
    turns = (total - ahead - first) // n

    def peeled(i):
        body(lambda k: At(i + k, (i + k) % n, (i + k) // n, total))

    for i in range(-ahead, first):
        peeled(i)
    with eng.Fori(0, turns) as r:
        if steps:
            steps.enter(r, per_turn)
        for u in range(n):
            body(lambda k: At(first + r * n + (u + k), (first + u + k) % n, r + (first + u + k) // n, total))
        if steps:
            steps.leave(turns, per_turn)
    for i in range(first + turns * n, total + behind):
        peeled(i)


def due(count):
    return not isinstance(count, int) or count > 0


def macaron(nc, batch, wq, bq, wk, bk, wv, bv, wo, bo, router, w_in_sh, w_out_sh, w_sw_sh,
            w_in_e, w_sw_e, w_out_e, out):
    B, S, D = batch.shape
    E, _, F = w_in_e.shape
    N = B * S
    T = N // P
    NB = T // BT
    W = BT * P
    G = S // P
    FC = F // P
    assert D == P and S == W and FC == 2 and E == 8
    CAP = N + P
    SLOTS = 8
    NT = -(-(TOPK * T + E - 1) // SLOTS) * SLOTS
    DUMMY = 8
    assert NT - TOPK * T <= DUMMY
    ROW = D + 1
    PADS = TOPK * N
    SCALE = float(D) ** -0.5

    x_t = batch.rearrange("b (j p) d -> p (b j) d", p=P)
    out_t = out.rearrange("b (j p) d -> p (b j) d", p=P)
    pairs = nc.dram_tensor("pairs", [E * CAP + DUMMY * P, ROW], F32).ap()
    results = nc.dram_tensor("results", [PADS + (E + DUMMY) * P, D], F32).ap()
    results_t = results[0:PADS, :].rearrange("(k t p) d -> p k t d", k=TOPK, p=P)

    with ExitStack() as ctx:
        def sb(name, shape, dt=F32):
            return ctx.enter_context(nc.sbuf_tensor(name, shape, dt))

        def sem(name):
            return ctx.enter_context(nc.semaphore(name))

        def sems(name, n):
            return [sem(f"{name}{i}") for i in range(n)]

        bank = [ctx.enter_context(nc.psum_tensor(f"bank{i}", [P, 512], F32)) for i in range(8)]

        X = sb("X", [P, T, D])
        XTR = sb("XTR", [P, N])
        XTH = sb("XTH", [P, 2, W], F32R)
        XTL = sb("XTL", [P, 2, W], F32R)
        WEH = sb("WEH", [P, E * 2 * F], F32R)
        WEL = sb("WEL", [P, E * 2 * F], F32R)
        WOE = sb("WOE", [P, E * FC * D])
        SHH = sb("SHH", [P, 2 * F], F32R)
        SHL = sb("SHL", [P, 2 * F], F32R)
        WOS = sb("WOS", [P, FC, D])
        WT4 = sb("WT4", [P, 4, D])
        RT = sb("RT", [P, E])
        bq_s = sb("bq_s", [P, 1])
        bk_s = sb("bk_s", [P, 1])
        bias_row = sb("bias_row", [1, 2, D])
        one_row = sb("one_row", [1, P])
        ident = sb("ident", [P, P])
        before = sb("before", [P, P], BF16)
        ones = sb("ones", [P, P], BF16)
        expert_no = sb("expert_no", [P, E])
        region = sb("region", [P, E])
        part_no = sb("part_no", [P, 1])
        dest = sb("dest", [P, TOPK, T], I32)
        pad_rows = sb("pad_rows", [P, E, ROW])
        pad_at = sb("pad_at", [P, E], U32)
        next_row = sb("next_row", [P, E])
        eps_c = sb("eps_c", [P, 1])
        ints = sb("ints", [P, E * 2], I32)
        tile_no = sb("tile_no", [1, NT])
        upto = sb("upto", [1, E, E])
        tile_i = sb("tile_i", [1, NT], I32)
        expert_of = sb("expert_of", [1, NT], I32)
        row_of = sb("row_of", [1, NT], I32)
        tcnt = sb("tcnt", [1, 4, E])
        tcnt_i = sb("tcnt_i", [1, 2, E], I32)
        tee = sb("tee", [1, E, E])
        tot_t = sb("tot_t", [1, 3, NT])
        XN = sb("XN", [P, 2, BT, D])
        XT32 = sb("XT32", [P, 2, W])
        ST = sb("ST", [P, 2, BT, 6])
        MV = sb("MV", [P, 2, BT, 2])
        SD = sb("SD", [P, 2, BT])
        RST = sb("RST", [P, 2, BT])
        SC = sb("SC", [P, BT, E])
        TOP = sb("TOP", [P, 2, BT, 8])
        TOPI = sb("TOPI", [P, BT, 8], U32)
        TNH = sb("TNH", [P, 2, BT, TOPK])
        GATE = sb("GATE", [P, 2, BT, TOPK])
        HOT = sb("HOT", [P, BT, TOPK, E])
        HOTB = sb("HOTB", [P, BT, E], BF16)
        RANK = sb("RANK", [P, BT, E])
        PICK = sb("PICK", [P, BT, TOPK, E])
        POS = sb("POS", [P, 2, BT, TOPK], U32)
        PAY = sb("PAY", [P, 2, TOPK, BT, ROW])
        arena = sb("arena", [P, 3584])

        def view(at, *shape):
            size = 1
            for n in shape:
                size *= n
            v = arena[:, at:at + size]
            if len(shape) == 1:
                return v
            names = "abc"[:len(shape)]
            return v.rearrange(f"p ({' '.join(names)}) -> p {' '.join(names)}", **dict(zip(names, shape)))

        XS = view(0, SLOTS, ROW)
        YO = view(SLOTS * ROW, SLOTS, D)
        SSG = view(0, FC, W)
        SHH_T = view(FC * W, 2, FC * W)
        AN = view(0, BT, D)
        AXT = view(512, W)
        QT = view(1024, W)
        KT = view(1536, W)
        PT = view(2048, 2, W)
        OT = view(3072, W)
        SHT = view(2048, 2 * F)
        XSH = sb("XSH", [P, 2, P], F32R)
        XSL = sb("XSL", [P, 2, P], F32R)
        SG = sb("SG", [P, 2, F])
        H = sb("H", [P, 2, F])
        HT = sb("HT", [P, 2, F])
        Y2 = sb("Y2", [P, 2, TOPK, BT, D])
        big = sb("big", [P, 2, BT, W])
        V = sb("V", [P, 2, G, D])
        NM = sb("NM", [P, 2, BT, G])
        SUM = sb("SUM", [P, 2, BT, G])
        R1 = sb("R1", [P, BT, G])
        R2 = sb("R2", [P, BT, G])
        R3 = sb("R3", [P, BT, 1])
        R4 = sb("R4", [P, BT, 1])

        vec = sem("vector_steps")
        act_s = sem("scalar_steps")
        pool_s = sem("pool_steps")
        k = dict((n, sem(n)) for n in (
            "weights_loaded small_loaded prep_transposed prep_read consts table_done pads_written "
            "normed xt_turned xt_copied xt_split scored topped tanh_done picked ranked "
            "rank_read gate_done pay0 pay1 placed up0 up1 silu0 silu1 hid0 hid1 down shared_added "
            "xs_turned xs_high xs_low e_up e_silu e_hid e_turned e_copied e_down e_out "
            "a_stats a_std a_normed a_turned a_copied q_made k_made v_made q_ready k_ready v_ready "
            "s_made m_ready probs_ready scaled t_even t_odd c_even c_odd av_made ot_ready proj_made updated "
            "carried_s carried_y kept_split r_stats r_std combined stored_y summed xt_high").split())
        x_loaded = sems("x_loaded", 2)
        y_loaded = sems("y_loaded", 2)
        scattered = sems("scattered", 2)
        xs_loaded = sems("xs_loaded", SLOTS)
        y_sent = sems("y_sent", SLOTS)
        stored = sems("stored", 2)

        def carry(dve, word=0):
            dve.memset(spare_v[:, word:word + 1], 0.0)

        def pool_carry(pool, which, n):
            if due(n):
                pool.wait_ge(k[which], n)
            word = spare_p[:, 0:1] if which == "carried_s" else spare_p[:, 1:2]
            pool.tensor_tensor(word, spare_p[:, 2:3], spare_p[:, 2:3], ALU.add).then_inc(k[which], 1)

        def x_block(b):
            return X[:, ds(BT * b.i, BT), :] if not isinstance(b.i, int) else X[:, BT * b.i:BT * b.i + BT, :]

        def cut(buf, at, size):
            return buf[:, at:at + size] if isinstance(at, int) else buf[:, ds(at, size)]

        def cols(buf, b):
            return cut(buf, BT * b.i, BT)

        def tile_of(buf, t):
            return buf[:, t:t + 1, :] if isinstance(t, int) else buf[:, ds(t, 1), :]

        def chunk(ap, j):
            return ap[:, j * P:(j + 1) * P]

        wst = view(0, 6, D)
        spare_v = sb("spare_v", [1, 5])
        spare_p = sb("spare_p", [1, 3])
        spare_a = sb("spare_a", [P, 1])
        vec_at = []
        stage = big[:, :, :, :].rearrange("p a b w -> p (a b w)")

        with nc.Block() as block:
            @block.sync
            def _(sp):
                for b in range(2):
                    sp.dma_start(X[:, BT * b:BT * b + BT, :], x_t[:, BT * b:BT * b + BT, :]).then_inc(x_loaded[b], 16)
                st3 = stage.rearrange("p (e g f) -> p e g f", e=E, g=2)
                sp.dma_start(st3[:, :, 0, :], w_in_e.rearrange("e d f -> d e f")).then_inc(k["weights_loaded"], 16)
                sp.dma_start(st3[:, :, 1, :], w_sw_e.rearrange("e d f -> d e f")).then_inc(k["weights_loaded"], 16)
                sp.dma_start(WOE[:, :].rearrange("p (e c d) -> p e c d", e=E, c=FC),
                             w_out_e.rearrange("e (c p) d -> p e c d", p=P)).then_inc(k["weights_loaded"], 16)
                sp.wait_ge(k["consts"], 1)
                sp.dma_start(pairs[E * CAP:E * CAP + DUMMY * P, :].rearrange("(e p) r -> p e r", p=P),
                             pad_rows[:, :, :]).then_inc(k["pads_written"], 16)
                sp.wait_ge(k["pads_written"], 16)

            @block.scalar
            def _(act):
                small = k["small_loaded"]
                act.dma_start(wst[:, 0:2, :],
                              w_in_sh.rearrange("(c p) d -> p c d", p=P)).then_inc(small, 16)
                act.dma_start(wst[:, 2:4, :], w_sw_sh.rearrange("(c p) d -> p c d", p=P)).then_inc(small, 16)
                act.dma_start(wst[:, 4:6, :].rearrange("p c d -> p (c d)"), w_out_sh).then_inc(small, 16)
                for n, w in enumerate((wq, wk, wv, wo)):
                    act.dma_start(XN[:, 0, n, :], w).then_inc(small, 16)
                act.dma_start(RT[:, :], router).then_inc(small, 16)
                act.dma_start(bq_s[:, :], bq.rearrange("(d a) -> d a", a=1)).then_inc(small, 16)
                act.dma_start(bk_s[:, :], bk.rearrange("(d a) -> d a", a=1)).then_inc(small, 16)
                act.dma_start(bias_row[:, 0, :], bv.rearrange("(a d) -> a d", a=1)).then_inc(small, 16)
                act.dma_start(bias_row[:, 1, :], bo.rearrange("(a d) -> a d", a=1)).then_inc(small, 16)
                act.wait_ge(small, 12 * 16)
                act.activation(bq_s[:, :], bq_s[:, :], ACT.Copy, scale=SCALE).then_inc(act_s, 1)

            @block.gpsimd
            def _(pool):
                st = Steps(pool, pool_s)
                for m, v in ((ident, 0.0), (before, 1.0), (ones, 1.0), (one_row, 1.0), (eps_c, EPS), (spare_p, 0.0), (pad_rows, 0.0),
                             (upto, 1.0)):
                    st.did(pool.memset(m[tuple(slice(None) for _ in m.shape)], v))
                st.did(pool.iota(ints[:, 0:E], pattern=[[P, E]], base=PADS + E * P, channel_multiplier=1))
                st.settle()
                st.did(pool.affine_select(out=ident[:, :], in_=ident[:, :], compare_op=ALU.not_equal, fill=1.0,
                                          base=0, pattern=[[-1, P]], channel_multiplier=1))
                st.did(pool.affine_select(out=before[:, :], in_=before[:, :], compare_op=ALU.is_gt, fill=0.0,
                                          base=0, pattern=[[1, P]], channel_multiplier=-1))
                st.did(pool.affine_select(out=upto[:, :, :], in_=upto[:, :, :], compare_op=ALU.is_ge, fill=0.0,
                                          base=0, pattern=[[1, E], [-1, E]], channel_multiplier=0))
                pool.tensor_copy(pad_rows[:, :, D:D + 1].bitcast(I32), ints[:, 0:E].unsqueeze(2)).then_inc(k["consts"], 1)
                st.did(pool.iota(dest[:, :, :], pattern=[[N, TOPK], [P, T]], base=0, channel_multiplier=1))
                st.did(pool.iota(tile_i[:, :], pattern=[[1, NT]], base=0, channel_multiplier=0))
                st.did(pool.iota(ints[:, E:2 * E], pattern=[[1, E]], base=0, channel_multiplier=0))
                st.settle()
                st.did(pool.tensor_copy(tile_no[:, :], tile_i[:, :]))
                st.did(pool.tensor_copy(expert_no[:, :], ints[:, E:2 * E]))
                pool.wait_ge(k["consts"], 1)
                st.settle()
                st.did(pool.iota(ints[:, 0:E], pattern=[[CAP, E]], base=0, channel_multiplier=0))
                st.settle()
                st.did(pool.tensor_copy(region[:, :], ints[:, 0:E]))
                st.did(pool.tensor_copy(next_row[:, :], ints[:, 0:E]))
                st.settle()
                st.did(pool.iota(ints[:, 0:1], pattern=[[0, 1]], base=0, channel_multiplier=1))
                st.settle()
                st.did(pool.tensor_copy(part_no[:, :], ints[:, 0:1]))
                st.settle()
                pool.wait_ge(k["pads_written"], 16)
                st.did(pool.iota(ints[:, 0:E], pattern=[[P, E]], base=PADS, channel_multiplier=1))
                st.settle()
                st.did(pool.tensor_copy(pad_rows[:, :, D:D + 1].bitcast(I32), ints[:, 0:E].unsqueeze(2)))
                st.settle()

            @block.tensor
            def _(pe):
                pe.wait_ge(k["small_loaded"], 12 * 16)
                pe.wait_ge(pool_s, 12)
                for c in range(4):
                    pe.transpose(chunk(bank[0], c), wst[:, c, :], ident[:, :])
                for n in range(4):
                    pe.transpose(chunk(bank[1], n), XN[:, 0, n, :], ident[:, :])
                for c in range(FC):
                    mm = pe.transpose(chunk(bank[2], c), wst[:, 4 + c, :], ident[:, :])
                mm.then_inc(k["prep_transposed"], 1)

            @block.vector
            def _(dve):
                st = Steps(dve, vec)
                dve.wait_ge(k["prep_transposed"], 1)
                st.did(dve.tensor_copy(SHT, bank[0][:, :]))
                st.did(dve.tensor_copy(WT4[:, :, :].rearrange("p n d -> p (n d)"), bank[1][:, :]))
                st.did(dve.tensor_copy(WOS[:, :, :].rearrange("p n d -> p (n d)"), bank[2][:, 0:F]))
                st.settle()
                st.did(dve.tensor_copy(SHH[:, :], SHT))
                st.settle()
                st.did(dve.tensor_tensor(SHL[:, :], SHT, SHH[:, :].bitcast(F32), ALU.subtract))
                st.settle()
                vec_at.append(st.n)

        def xt_bank(done):
            return bank[3 if done else 0]

        def score_bank(done):
            return bank[1 if done else 7]

        def pe_route(pe, b, done):
            n = done + b.i
            pe.wait_ge(k["normed"], n + 1)
            if due(n):
                pe.wait_ge(k["xt_copied"], n)
            if done == 0 and due(n):
                pe.wait_ge(k["xt_high"], n)
            if done:
                pe.wait_ge(k["updated"], b.i + 2 if not isinstance(b.i, int) else min(b.i + 2, NB))
            for j in range(BT):
                mm = pe.transpose(chunk(xt_bank(done), j), XN[:, b.buf, j, :], ident[:, :])
            mm.then_inc(k["xt_turned"], 1)

        def pe_score(pe, b, done):
            n = done + b.i
            pe.wait_ge(k["xt_copied"], n + 1)
            if done and due(n):
                pe.wait_ge(k["rank_read"], n)
            if not done and due(n):
                pe.wait_ge(k["topped"], n)
            for j in range(BT):
                mm = pe.matmul(score_bank(done)[:, j * E:(j + 1) * E], XT32[:, b.buf, j * P:(j + 1) * P], RT[:, :],
                               start=True, stop=True)
            mm.then_inc(k["scored"], 1)

        def pe_rank(pe, b, done):
            pe.wait_ge(k["picked"], done + b.i + 1)
            rk = bank[1][:, 0:BT * E]
            hot = HOTB[:, :, :].rearrange("p j e -> p (j e)")
            pe.matmul(rk, before[:, :], hot, start=True, stop=False)
            for s in range(1, BT):
                pe.matmul(rk[:, s * E:], ones[:, :], hot[:, 0:(BT - s) * E], start=False, stop=(s == BT - 1))
            tot = bank[1][:, BT * E:(BT + 1) * E]
            for j in range(BT):
                mm = pe.matmul(tot, ones[:, :], hot[:, j * E:(j + 1) * E], start=(j == 0), stop=(j == BT - 1))
            mm.then_inc(k["ranked"], 1)

        def act_copy_xt(act, b, done):
            n = done + b.i
            act.wait_ge(k["xt_turned"], n + 1)
            if due(n - 1):
                act.wait_ge(k["scored"], n - 1)
            if due(n - 1):
                act.wait_ge(k["xt_split"], n - 1)
            act.activation(XT32[:, b.buf, :], xt_bank(done)[:, :], ACT.Copy).then_inc(k["xt_copied"], 1)

        def act_gates(act, b, done):
            n = done + b.i
            act.wait_ge(k["topped"], n + 1)
            if due(n - 1):
                act.wait_ge(k["gate_done"], n - 1)
            act.activation(TNH[:, b.buf, :, :], TOP[:, b.buf, :, 0:TOPK], ACT.Tanh, scale=0.5)\
               .then_inc(k["tanh_done"], 1)

        def act_payload(act, b, done):
            n = done + b.i
            act.wait_ge(k["gate_done"], n + 1)
            if due(BT * TOPK * 16 * (done // 2 + b.uses)):
                act.wait_ge(scattered[b.buf], BT * TOPK * 16 * (done // 2 + b.uses))
            for j in range(BT):
                ins = act.activation(PAY[:, b.buf, 1, j, 0:D], XN[:, b.buf, j, :], ACT.Copy,
                                     scale=GATE[:, b.buf, j, 1:2])
            ins.then_inc(k["pay1"], 1)

        def dve_moments(dve, st, b, which, sem_, count):
            dve.wait_ge(sem_, count)
            carry(dve, 1 + which)
            for j in range(BT):
                st.did(dve.bn_stats(ST[:, which, j, :], tile_of(X, BT * b.i + j).rearrange("p a d -> p (a d)")))
            return st.mark()

        def dve_mean_var(dve, st, b, which, after, name, done):
            dve.wait_ge(*after)
            carry(dve, 3 + which)
            for j in range(BT):
                ins = dve.bn_aggr(MV[:, which, j, :], ST[:, which, j, :])
            st.signals(ins, k[name], done + b.i + 1)

        def act_std(act, b, which, stats, name, done):
            act.wait_ge(k[stats], done + b.i + 1)
            act.activation(SD[:, which, :], MV[:, which, :, 1], ACT.Sqrt, bias=eps_c[:, :]).then_inc(k[name], 1)

        def dve_rstd(dve, st, b, which, name, done):
            dve.wait_ge(k[name], done + b.i + 1)
            st.did(dve.reciprocal(RST[:, which, :], SD[:, which, :]))
            return st.mark()

        def dve_norm(dve, st, b, done):
            n = done + b.i
            if due(n - 1):
                dve.wait_ge(k["xt_turned"], n - 1)
            if due(n - 1):
                dve.wait_ge(k["pay1"], n - 1)
            for j in range(BT):
                t = BT * b.i + j
                ins = dve.tensor_scalar(XN[:, b.buf, j:j + 1, :], tile_of(X, t), MV[:, 1, j, 0:1],
                                        RST[:, 1, j:j + 1], ALU.subtract, ALU.mult)
            st.signals(ins, k["normed"], n + 1)

        def act_high(act, b):
            if due(b.i - 1):
                act.wait_ge(k["up1"], b.i - 1)
            act.activation(XTH[:, b.buf, :], xt_bank(0)[:, :], ACT.Copy).then_inc(k["xt_high"], 1)

        def dve_low(dve, st, b):
            dve.wait_ge(k["xt_high"], b.i + 1)
            if due(b.i - 1):
                dve.wait_ge(k["up1"], b.i - 1)
            st.signals(dve.tensor_tensor(XTL[:, b.buf, :], XT32[:, b.buf, :], XTH[:, b.buf, :].bitcast(F32),
                                         ALU.subtract), k["xt_split"], b.i + 1)

        def dve_split_kept(dve, st, b):
            if due(NB + b.i - 1):
                dve.wait_ge(k["up1"], NB + b.i - 1)
            hi, lo = XTH[:, b.buf, :], XTL[:, b.buf, :]
            st.did(dve.tensor_copy(hi, cut(XTR, W * b.i, W)))
            st.settle()
            st.signals(dve.tensor_tensor(lo, cut(XTR, W * b.i, W), hi.bitcast(F32), ALU.subtract), k["kept_split"], b.i + 1)

        def dve_top(dve, st, b, done):
            n = done + b.i
            dve.wait_ge(k["scored"], n + 1)
            st.did(dve.tensor_copy(SC[:, :, :].rearrange("p j e -> p (j e)"), score_bank(done)[:, 0:BT * E]))
            st.settle()
            if due(n - 1):
                dve.wait_ge(k["tanh_done"], n - 1)
            carry(dve)
            for j in range(BT):
                ins = dve.max(TOP[:, b.buf, j, :], SC[:, j, :])
            st.signals(ins, k["topped"], n + 1)
            st.settle()
            carry(dve)
            for j in range(BT):
                st.did(dve.max_index(TOPI[:, j, :], TOP[:, b.buf, j, :], SC[:, j, :]))
            st.settle()
            st.did(dve.tensor_tensor(HOT[:, :, :, :],
                                     TOPI[:, :, 0:TOPK].unsqueeze(3).to_broadcast([P, BT, TOPK, E]),
                                     expert_no[:, :].unsqueeze(1).unsqueeze(1).to_broadcast([P, BT, TOPK, E]),
                                     ALU.is_equal))
            st.settle()
            st.signals(dve.tensor_tensor(HOTB[:, :, :], HOT[:, :, 0, :], HOT[:, :, 1, :], ALU.add), k["picked"], n + 1)

        def dve_payload(dve, st, b, done):
            n = done + b.i
            dve.wait_ge(k["tanh_done"], n + 1)
            if due(BT * TOPK * 16 * (done // 2 + b.uses)):
                dve.wait_ge(scattered[b.buf], BT * TOPK * 16 * (done // 2 + b.uses))
            st.signals(dve.tensor_scalar(GATE[:, b.buf, :, :], TNH[:, b.buf, :, :], 0.5, 0.5, ALU.mult, ALU.add), k["gate_done"], n + 1)
            where = dest[:, :, BT * b.i:BT * b.i + BT] if isinstance(b.i, int) else dest[:, :, ds(BT * b.i, BT)]
            st.did(dve.tensor_copy(PAY[:, b.buf, :, :, D:D + 1].bitcast(I32), where.unsqueeze(3)))
            st.settle()
            for j in range(BT):
                ins = dve.tensor_scalar(PAY[:, b.buf, 0, j, 0:D], XN[:, b.buf, j, :],
                                               GATE[:, b.buf, j, 0:1], None, ALU.mult)
            st.signals(ins, k["pay0"], n + 1)

        def dve_place(dve, st, b, done):
            dve.wait_ge(k["ranked"], done + b.i + 1)
            st.did(dve.tensor_tensor(RANK[:, :, :], bank[1][:, 0:BT * E].rearrange("p (j e) -> p j e", e=E),
                                     next_row[:, :].unsqueeze(1).to_broadcast([P, BT, E]), ALU.add))
            st.settle()
            st.signals(dve.tensor_tensor(next_row[:, :], bank[1][:, BT * E:(BT + 1) * E], next_row[:, :], ALU.add), k["rank_read"], done + b.i + 1)
            st.did(dve.tensor_tensor(PICK[:, :, :, :], HOT[:, :, :, :],
                                     RANK[:, :, :].unsqueeze(2).to_broadcast([P, BT, TOPK, E]), ALU.mult))
            st.settle()
            with nc.allow_low_precision(reason="row numbers: whole, below 2^24"):
                st.signals(dve.tensor_reduce(POS[:, b.buf, :, :], PICK[:, :, :, :], AXX, ALU.add), k["placed"], done + b.i + 1)

        def pool_scatter(pool, b, done):
            n = done + b.i
            pool.wait_ge(k["pay0"], n + 1)
            pool.wait_ge(k["pay1"], n + 1)
            pool.wait_ge(k["placed"], n + 1)
            pool_carry(pool, "carried_s", n)
            for j in range(BT):
                for c in range(TOPK):
                    pool.indirect_dma_start(pairs, bass.IndirectOffsetOnAxis(ap=POS[:, b.buf, j, c:c + 1], axis=0),
                                            PAY[:, b.buf, c, j, :], None).then_inc(scattered[b.buf], 16)

        def pe_shared_up(pe, b, done):
            n = done + b.i
            pe.wait_ge(k["xt_split" if done == 0 else "kept_split"], b.i + 1)
            hi, lo = XTH[:, b.buf, :], XTL[:, b.buf, :]
            for c in range(FC):
                if due(n):
                    pe.wait_ge(k[f"hid{c}"], n)
                for g in range(2):
                    ps = bank[2 + 2 * c + g]
                    w = slice(g * F + c * P, g * F + (c + 1) * P)
                    pe.matmul(ps[:, :], SHL[:, w], hi, start=True, stop=False)
                    pe.matmul(ps[:, :], SHH[:, w], lo, start=False, stop=False)
                    mm = pe.matmul(ps[:, :], SHH[:, w], hi, start=False, stop=True)
                mm.then_inc(k[f"up{c}"], 1)

        def act_shared(act, b, done):
            n = done + b.i
            for c in range(FC):
                act.wait_ge(k[f"up{c}"], n + 1)
                if due(n):
                    act.wait_ge(k[f"hid{c}"], n)
                act.activation(SSG[:, c, :], bank[2 + 2 * c][:, :], ACT.Silu).then_inc(k[f"silu{c}"], 1)

        def dve_shared_mul(dve, st, b, done):
            n = done + b.i
            if due(n - 1):
                dve.wait_ge(k["down"], n - 1)
            for c in range(FC):
                dve.wait_ge(k[f"silu{c}"], n + 1)
                st.signals(dve.tensor_tensor(SHH_T[:, b.buf, c * W:(c + 1) * W], bank[3 + 2 * c][:, :], SSG[:, c, :], ALU.mult), k[f"hid{c}"], n + 1)

        def pe_shared_down(pe, b, done):
            n = done + b.i
            pe.wait_ge(k["hid0"], n + 1)
            pe.wait_ge(k["hid1"], n + 1)
            if due(n):
                pe.wait_ge(k["shared_added"], n)
            for j in range(BT):
                for c in range(FC):
                    mm = pe.matmul(chunk(bank[6], j), SHH_T[:, b.buf, c * W + j * P:c * W + (j + 1) * P], WOS[:, c, :],
                                   start=(c == 0), stop=(c == FC - 1))
            mm.then_inc(k["down"], 1)

        def dve_shared_add(dve, st, b, done):
            dve.wait_ge(k["down"], done + b.i + 1)
            st.signals(dve.scalar_tensor_tensor(out=x_block(b), in0=bank[6][:, :].rearrange("p (j d) -> p j d", d=D),
                                            scalar=0.5, in1=x_block(b), op0=ALU.mult, op1=ALU.add), k["shared_added"], done + b.i + 1)

        with nc.Block() as block:
            @block.sync
            def _(sp):
                with sp.Fori(1, NB // 2) as r:
                    for u in range(2):
                        sp.wait_ge(x_loaded[u], 16 * r)
                        sp.dma_start(X[:, ds(2 * BT * r + BT * u, BT), :],
                                     x_t[:, ds(2 * BT * r + BT * u, BT), :]).then_inc(x_loaded[u], 16)

            @block.vector
            def _(dve):
                st = Steps(dve, vec, vec_at[0])

                def body(at):
                    ahead, new, b, c = at(2), at(1), at(0), at(-1)
                    if new.live:
                        rst = dve_rstd(dve, st, new, 1, "r_std", 0)
                    if new.live:
                        dve.wait_ge(*rst)
                        dve_norm(dve, st, new, 0)
                    if b.live:
                        dve_top(dve, st, b, 0)
                        dve_shared_mul(dve, st, b, 0)
                    if new.live:
                        dve_low(dve, st, new)
                    if ahead.live:
                        seen = dve_moments(dve, st, ahead, 1, x_loaded[ahead.buf], 16 * (ahead.uses + 1))
                    if b.live:
                        dve_payload(dve, st, b, 0)
                    if ahead.live:
                        dve_mean_var(dve, st, ahead, 1, seen, "r_stats", 0)
                    if b.live:
                        dve_place(dve, st, b, 0)
                    if c.live:
                        dve_shared_add(dve, st, c, 0)
                    if isinstance(b.i, int) and b.i == 0:
                        dve.wait_ge(k["weights_loaded"], 48)
                        st.did(dve.tensor_copy(WEH[:, :], stage))
                        st.settle()
                        st.did(dve.tensor_tensor(WEL[:, :], stage, WEH[:, :].bitcast(F32), ALU.subtract))
                        st.settle()
                rolled(dve, NB, 2, 1, body, st, 2 * 14)
                vec_at[0] = st.base + st.n

            @block.scalar
            def _(act):
                def body(at):
                    ahead, new, b = at(2), at(1), at(0)
                    if b.live:
                        act_shared(act, b, 0)
                        act_gates(act, b, 0)
                    if new.live:
                        act_copy_xt(act, new, 0)
                        act_high(act, new)
                    if b.live:
                        act_payload(act, b, 0)
                    if ahead.live:
                        act_std(act, ahead, 1, "r_stats", "r_std", 0)
                    act.activation(spare_a[:, :], eps_c[:, :], ACT.Silu)
                rolled(act, NB, 2, 0, body)

            @block.tensor
            def _(pe):
                def body(at):
                    new, b, c = at(1), at(0), at(-1)
                    if b.live:
                        pe_shared_up(pe, b, 0)
                    if new.live:
                        pe_route(pe, new, 0)
                    if c.live:
                        pe_shared_down(pe, c, 0)
                    if b.live:
                        pe_rank(pe, b, 0)
                    if new.live:
                        pe_score(pe, new, 0)
                rolled(pe, NB, 1, 1, body)

            @block.gpsimd
            def _(pool):
                rolled(pool, NB, 0, 0, lambda at: pool_scatter(pool, at(0), 0))
                for s in scattered:
                    pool.wait_ge(s, BT * TOPK * 16 * NB // 2)

        def experts(done):
            first = done == 0
            ffn = 0 if first else 1
            with nc.Block() as block:
                @block.vector
                def _(dve):
                    st = Steps(dve, vec, vec_at[0])
                    st.did(dve.tensor_scalar(pad_at[:, :], next_row[:, :], part_no[:, :], None, ALU.add))
                    cnt, tiles, ends = tcnt[:, 0, :], tcnt[:, 1, :], tcnt[:, 2, :]
                    st.did(dve.tensor_tensor(cnt, next_row[0:1, :], region[0:1, :], ALU.subtract))
                    st.settle()
                    st.did(dve.tensor_scalar(tcnt_i[:, 0, :], cnt, float(P - 1), None, ALU.add))
                    st.settle()
                    st.did(dve.tensor_scalar(tcnt_i[:, 1, :], tcnt_i[:, 0, :], 7, None, ALU.arith_shift_right))
                    st.settle()
                    st.did(dve.tensor_copy(tiles, tcnt_i[:, 1, :]))
                    st.settle()
                    st.did(dve.tensor_tensor(tee[:, :, :], upto[:, :, :], tiles.unsqueeze(1).to_broadcast([1, E, E]), ALU.mult))
                    st.settle()
                    st.did(dve.tensor_reduce(ends, tee[:, :, :], AXX, ALU.add))
                    st.settle()
                    tbl = big[0:1, 0, :, :].rearrange("p a w -> p (a w)")[:, 0:NT * E].rearrange("p (t e) -> p t e", e=E)
                    st.did(dve.tensor_tensor(tbl, tile_no[:, :].unsqueeze(2).to_broadcast([1, NT, E]),
                                             ends.unsqueeze(1).to_broadcast([1, NT, E]), ALU.is_ge))
                    st.settle()
                    ex, gone, row = tot_t[:, 0, :], tot_t[:, 1, :], tot_t[:, 2, :]
                    st.did(dve.tensor_reduce(ex, tbl, AXX, ALU.add))
                    st.settle()
                    st.did(dve.tensor_tensor(tbl, tbl, tiles.unsqueeze(1).to_broadcast([1, NT, E]), ALU.mult))
                    st.settle()
                    st.did(dve.tensor_reduce(gone, tbl, AXX, ALU.add))
                    st.did(dve.tensor_scalar(expert_of[:, :], ex, float(E - 1), None, ALU.min))
                    st.settle()
                    st.did(dve.tensor_tensor(row, tile_no[:, :], gone, ALU.subtract))
                    st.did(dve.tensor_scalar(ex, ex, float(CAP), None, ALU.mult))
                    st.settle()
                    st.did(dve.scalar_tensor_tensor(out=row_of[:, :], in0=row, scalar=float(P), in1=ex,
                                                    op0=ALU.mult, op1=ALU.add))
                    st.signals(dve.tensor_copy(next_row[:, :], region[:, :]), k["table_done"], ffn + 1)
                    st.settle()

                    def body(at):
                        nx, t, od = at(2), at(0), at(-2)
                        if t.live:
                            dve.wait_ge(k["e_silu"], done + t.i + 1)
                            if due(done + t.i - 1):
                                dve.wait_ge(k["e_turned"], done + t.i - 1)
                            st.signals(dve.tensor_tensor(H[:, t.buf % 2, :], bank[2 + t.buf % 2][:, F:2 * F],
                                                     SG[:, t.buf % 2, :], ALU.mult), k["e_hid"], done + t.i + 1)
                        if od.live:
                            dve.wait_ge(k["e_down"], done + od.i + 1)
                            if due(16 * (done // SLOTS + od.uses)):
                                dve.wait_ge(y_sent[od.buf], 16 * (done // SLOTS + od.uses))
                            st.signals(dve.tensor_scalar(YO[:, od.buf, :], bank[6 + od.buf % 2][:, 0:D], 0.5, None,
                                                     ALU.mult), k["e_out"], done + od.i + 1)
                        if nx.live:
                            dve.wait_ge(k["xs_high"], done + nx.i + 1)
                            if due(done + nx.i - 1):
                                dve.wait_ge(k["e_up"], done + nx.i - 1)
                            st.signals(dve.tensor_tensor(XSL[:, nx.buf % 2, :], bank[nx.buf % 2][:, 0:P],
                                                     XSH[:, nx.buf % 2, :].bitcast(F32), ALU.subtract), k["xs_low"], done + nx.i + 1)
                    rolled(dve, NT, 2, 2, body, st, 0, n=SLOTS, peel=SLOTS)
                    vec_at[0] = st.base + st.n

                @block.gpsimd
                def _(pool):
                    pool.wait_ge(k["table_done"], ffn + 1)
                    for e in range(E):
                        pool.indirect_dma_start(pairs, bass.IndirectOffsetOnAxis(ap=pad_at[:, e:e + 1], axis=0),
                                                pad_rows[:, e, :], None).then_inc(k["stored_y"], 16)

                    def send(at):
                        t = at(0)
                        pool.wait_ge(k["e_out"], done + t.i + 1)
                        pool_carry(pool, "carried_y", done + t.i)
                        pool.indirect_dma_start(
                            results, bass.IndirectOffsetOnAxis(ap=XS[:, t.buf, D:D + 1].bitcast(U32), axis=0),
                            YO[:, t.buf, :], None).then_inc(y_sent[t.buf], 16)
                    rolled(pool, NT, 0, 0, send, n=SLOTS)
                    for s in y_sent:
                        pool.wait_ge(s, 16 * (done + NT) // SLOTS)

                @block.sync
                def _(sp):
                    sp.wait_ge(k["table_done"], ffn + 1)
                    sp.wait_ge(k["stored_y"], 16 * E * (ffn + 1))
                    rows = [sp.alloc_register(f"row{ffn}_{i}") for i in range(SLOTS)]
                    def load(r):
                        sp.reg_load(rows, row_of[0:1, ds(r * SLOTS, SLOTS)])
                        for u in range(SLOTS):
                            row = sp.snap(rows[u], min_val=0, max_val=E * CAP + (DUMMY - 1) * P)
                            if due((r + done // SLOTS) * 16):
                                sp.wait_ge(y_sent[u], (r + done // SLOTS) * 16)
                            sp.dma_start(XS[:, u, :], pairs[ds(row, P), :]).then_inc(xs_loaded[u], 16)
                    load(0)
                    with sp.Fori(1, NT // SLOTS) as r:
                        load(r)

                @block.scalar
                def _(act):
                    def body(at):
                        nx, t, ld = at(2), at(0), at(-1)
                        if t.live:
                            act.wait_ge(k["e_up"], done + t.i + 1)
                            if due(done + t.i - 1):
                                act.wait_ge(k["e_hid"], done + t.i - 1)
                            act.activation(SG[:, t.buf % 2, :], bank[2 + t.buf % 2][:, 0:F], ACT.Silu)\
                               .then_inc(k["e_silu"], 1)
                        if ld.live:
                            act.wait_ge(k["e_turned"], done + ld.i + 1)
                            if due(done + ld.i - 1):
                                act.wait_ge(k["e_down"], done + ld.i - 1)
                            act.activation(HT[:, ld.buf % 2, :], bank[4 + ld.buf % 2][:, 0:F], ACT.Copy)\
                               .then_inc(k["e_copied"], 1)
                        if nx.live:
                            act.wait_ge(k["xs_turned"], done + nx.i + 1)
                            if due(done + nx.i - 1):
                                act.wait_ge(k["e_up"], done + nx.i - 1)
                            act.activation(XSH[:, nx.buf % 2, :], bank[nx.buf % 2][:, 0:P], ACT.Copy)\
                               .then_inc(k["xs_high"], 1)
                    rolled(act, NT, 2, 1, body, n=SLOTS)

                @block.tensor
                def _(pe):
                    pe.wait_ge(k["table_done"], ffn + 1)
                    regs = [pe.alloc_register(f"expert{ffn}_{i}") for i in range(SLOTS + 2)]

                    def expert(reg):
                        return pe.snap(reg, min_val=0, max_val=E - 1)

                    def body(nx, t, ld, od, up_reg, down_reg):
                        if t.live:
                            e = expert(up_reg)
                            ps = bank[2 + t.buf % 2][:, :]
                            hi, lo = XSH[:, t.buf % 2, :], XSL[:, t.buf % 2, :]
                            pe.wait_ge(k["xs_low"], done + t.i + 1)
                            if due(done + t.i - 1):
                                pe.wait_ge(k["e_hid"], done + t.i - 1)
                            pe.matmul(ps, lo, WEH[:, ds(e * 2 * F, 2 * F)], start=True, stop=False)
                            pe.matmul(ps, hi, WEL[:, ds(e * 2 * F, 2 * F)], start=False, stop=False)
                            pe.matmul(ps, hi, WEH[:, ds(e * 2 * F, 2 * F)], start=False, stop=True)\
                              .then_inc(k["e_up"], 1)
                        if od.live:
                            e = expert(down_reg)
                            pe.wait_ge(k["e_copied"], done + od.i + 1)
                            if due(done + od.i - 1):
                                pe.wait_ge(k["e_out"], done + od.i - 1)
                            for c in range(FC):
                                mm = pe.matmul(bank[6 + od.buf % 2][:, 0:D], HT[:, od.buf % 2, c * P:(c + 1) * P],
                                               WOE[:, ds(e * FC * D + c * D, D)], start=(c == 0), stop=(c == FC - 1))
                            mm.then_inc(k["e_down"], 1)
                        if ld.live:
                            pe.wait_ge(k["e_hid"], done + ld.i + 1)
                            if due(done + ld.i - 1):
                                pe.wait_ge(k["e_copied"], done + ld.i - 1)
                            for c in range(FC):
                                mm = pe.transpose(chunk(bank[4 + ld.buf % 2], c), H[:, ld.buf % 2, c * P:(c + 1) * P],
                                                  ident[:, :])
                            mm.then_inc(k["e_turned"], 1)
                        if nx.live:
                            pe.wait_ge(xs_loaded[nx.buf], 16 * (done // SLOTS + nx.uses + 1))
                            if due(done + nx.i - 1):
                                pe.wait_ge(k["xs_low"], done + nx.i - 1)
                            pe.transpose(bank[nx.buf % 2][:, 0:P], XS[:, nx.buf, 0:D], ident[:, :])\
                              .then_inc(k["xs_turned"], 1)

                    def some(lo, hi):
                        of = range(max(lo - 2, 0), min(hi, NT))
                        pe.reg_load(regs[:len(of)], expert_of[0:1, of[0]:of[-1] + 1])
                        for i in range(lo, hi):
                            def at(d):
                                return At(i + d, (i + d) % SLOTS, (i + d) // SLOTS, NT)
                            body(at(2), at(0), at(-1), at(-2), regs[of.index(i)] if i in of else None,
                                 regs[of.index(i - 2)] if i - 2 in of else None)

                    turns = (NT - 6) // SLOTS
                    some(-2, 4)
                    with pe.Fori(0, turns) as r:
                        pe.reg_load(regs, expert_of[0:1, ds(r * SLOTS + 2, SLOTS + 2)])
                        for u in range(SLOTS):
                            def at(d):
                                return At(r * SLOTS + (4 + u + d), (4 + u + d) % SLOTS, r + (4 + u + d) // SLOTS, NT)
                            body(at(2), at(0), at(-1), at(-2), regs[u + 2], regs[u])
                    some(4 + turns * SLOTS, NT + 2)

        experts(0)

        def load_y(sp, b, done):
            if due(done + b.i - 1):
                sp.wait_ge(k["combined"], done + b.i - 1)
            src = results_t[:, :, BT * b.i:BT * b.i + BT, :] if isinstance(b.i, int) else results_t[:, :, ds(BT * b.i, BT), :]
            for c in range(TOPK):
                sp.dma_start(Y2[:, b.buf, c, :, :], src[:, c, :, :]).then_inc(y_loaded[b.buf], 8 * 2)

        def up_to(b, more):
            return b.i + more if not isinstance(b.i, int) else min(b.i + more, NB)

        with nc.Block() as block:
            @block.sync
            def _(sp):
                rolled(sp, NB, 0, 0, lambda at: load_y(sp, at(0), 0))

            @block.vector
            def _(dve):
                st = Steps(dve, vec, vec_at[0])

                def maximum(b, a):
                    dve.wait_ge(k["s_made"], BT * b.i + (a + 1))
                    if a == 0 and due(BT * b.i - BT):
                        dve.wait_ge(k["probs_ready"], BT * b.i - BT)
                    st.signals(dve.tensor_reduce(NM[:, b.buf, a, :],
                                                 bank[4 + a % 2][:, :].rearrange("p (g c) -> p g c", c=P),
                                                 AXX, ALU.max, negate=True), k["m_ready"], BT * b.i + (a + 1))

                def normalise(new):
                    if due(new.i):
                        dve.wait_ge(k["a_turned"], new.i)
                    for j in range(BT):
                        ins = dve.tensor_scalar(AN[:, j:j + 1, :], tile_of(X, BT * new.i + j),
                                                MV[:, 0, j, 0:1], RST[:, 0, j:j + 1],
                                                ALU.subtract, ALU.mult)
                    st.signals(ins, k["a_normed"], new.i + 1)

                def add_result(b):
                    dve.wait_ge(k["summed"], b.i + 1)
                    st.signals(dve.tensor_tensor(x_block(b), x_block(b), Y2[:, b.buf, 0, :, :], ALU.add),
                               k["combined"], b.i + 1)
                    return st.mark()

                def update(c):
                    dve.wait_ge(k["proj_made"], c.i + 1)
                    st.signals(dve.tensor_tensor(x_block(c), bank[3][:, :].rearrange("p (j d) -> p j d", d=D),
                                                 x_block(c), ALU.add), k["updated"], c.i + 1)
                    return st.mark()

                def weight(b, n, after):
                    dve.wait_ge(*after)
                    sm = SUM[:, b.buf, :, :]
                    if n == 0:
                        ins = dve.reciprocal(R1[:, :, :], sm)
                    elif n == 1:
                        ins = dve.tensor_tensor(R2[:, :, :], R1[:, :, :], sm, ALU.mult)
                    elif n == 2:
                        ins = dve.tensor_reduce(R3[:, :, :], R2[:, :, :].unsqueeze(2), AXX, ALU.add)
                    elif n == 3:
                        ins = dve.tensor_scalar(R3[:, :, :], R3[:, :, :], 1e-6, None, ALU.add)
                    elif n == 4:
                        ins = dve.reciprocal(R4[:, :, :], R3[:, :, :])
                    else:
                        ins = dve.tensor_tensor(R2[:, :, :], R1[:, :, :], R4[:, :, :].to_broadcast([P, BT, G]),
                                                ALU.mult)
                    st.did(ins)
                    return st.mark()

                def scale(b, a):
                    e3 = big[:, b.buf, a, :].rearrange("p (g c) -> p g c", c=P)
                    st.signals(dve.tensor_tensor(e3, e3, R2[:, a, :].unsqueeze(2).to_broadcast([P, G, P]),
                                                 ALU.mult), k["scaled"], BT * b.i + (a + 1))

                def body(at):
                    ahead, new, b, c, upd, old, out = (at(d) for d in range(2, -5, -1))
                    if b.live:
                        maximum(b, 0)
                        maximum(b, 1)
                    if c.live:
                        st.settle()
                        for a in range(BT):
                            scale(c, a)
                    if new.live:
                        rst_new = dve_rstd(dve, st, new, 0, "a_std", 0)
                    if old.live:
                        rst_old = dve_rstd(dve, st, old, 1, "r_std", NB)
                    if new.live:
                        dve.wait_ge(*rst_new)
                        normalise(new)
                    if b.live:
                        maximum(b, 2)
                    if upd.live:
                        updated = update(upd)
                    if old.live:
                        dve.wait_ge(*rst_old)
                        dve_norm(dve, st, old, NB)
                    if b.live:
                        maximum(b, 3)
                    if out.live:
                        dve_payload(dve, st, out, NB)
                        dve_place(dve, st, out, NB)
                    if ahead.live:
                        added = add_result(ahead)
                    if b.live:
                        r1 = weight(b, 0, (k["probs_ready"], BT * (b.i + 1)))
                    if upd.live:
                        seen_u = dve_moments(dve, st, upd, 1, *updated)
                    if b.live:
                        r2 = weight(b, 1, r1)
                    if ahead.live:
                        seen = dve_moments(dve, st, ahead, 0, *added)
                    if b.live:
                        r3 = weight(b, 2, r2)
                    if upd.live:
                        dve_mean_var(dve, st, upd, 1, seen_u, "r_stats", NB)
                    if b.live:
                        r3 = weight(b, 3, r3)
                    if ahead.live:
                        dve_mean_var(dve, st, ahead, 0, seen, "a_stats", 0)
                    if b.live:
                        r4 = weight(b, 4, r3)
                        weight(b, 5, r4)
                    if old.live:
                        dve_top(dve, st, old, NB)
                rolled(dve, NB, 2, 4, body, st, 2 * 25)
                vec_at[0] = st.base + st.n

            @block.scalar
            def _(act):
                def exps(b, a):
                    act.wait_ge(k["m_ready"], BT * b.i + (a + 1))
                    if a == 0 and due(2 * (b.i - 1)):
                        act.wait_ge(k["t_odd"], 2 * (b.i - 1))
                    for g in range(G):
                        ins = act.activation(big[:, b.buf, a, g * P:(g + 1) * P], chunk(bank[4 + a % 2], g),
                                             ACT.Exp, bias=NM[:, b.buf, a, g:g + 1],
                                             accum_out=SUM[:, b.buf, a, g:g + 1])
                    ins.then_inc(k["probs_ready"], 1)

                def copy_turned(c, g):
                    h = g // 2
                    if g % 2 == 0:
                        act.wait_ge(k["t_even"], 2 * c.i + (h + 1))
                        if due(2 * (2 * c.i + h) - 1):
                            act.wait_ge(k["av_made"], 2 * (2 * c.i + h) - 1)
                        act.activation(PT[:, 0, :], bank[6][:, :], ACT.Copy).then_inc(k["c_even"], 1)
                    else:
                        act.wait_ge(k["t_odd"], 2 * c.i + (h + 1))
                        if due(2 * (2 * c.i + h)):
                            act.wait_ge(k["av_made"], 2 * (2 * c.i + h))
                        act.activation(PT[:, 1, :], bank[7][:, :], ACT.Copy).then_inc(k["c_odd"], 1)

                def body(at):
                    new, b, c, old, out = at(1), at(0), at(-1), at(-3), at(-4)
                    if new.live:
                        act_std(act, new, 0, "a_stats", "a_std", 0)
                    if old.live:
                        act_std(act, old, 1, "r_stats", "r_std", NB)
                    if out.live:
                        act_gates(act, out, NB)
                    if b.live:
                        exps(b, 0)
                        exps(b, 1)
                        act.wait_ge(k["v_made"], b.i + 1)
                        if due(4 * (b.i - 1)):
                            act.wait_ge(k["av_made"], 4 * (b.i - 1))
                        act.activation(V[:, b.buf, :, :].rearrange("p g d -> p (g d)"), bank[0][:, :], ACT.Copy)\
                           .then_inc(k["v_ready"], 1)
                        exps(b, 2)
                    if c.live:
                        copy_turned(c, 0)
                        copy_turned(c, 1)
                    if b.live:
                        exps(b, 3)
                    if c.live:
                        copy_turned(c, 2)
                    if new.live:
                        act.wait_ge(k["a_turned"], new.i + 1)
                        if due(new.i):
                            act.wait_ge(k["v_made"], new.i)
                        act.activation(AXT, bank[0][:, :], ACT.Copy).then_inc(k["a_copied"], 1)
                    if c.live:
                        copy_turned(c, 3)
                    if new.live:
                        act.wait_ge(k["q_made"], new.i + 1)
                        if due(BT * new.i):
                            act.wait_ge(k["s_made"], BT * new.i)
                        act.activation(QT, bank[4][:, :], ACT.Identity, bias=bq_s[:, :], scale=SCALE)\
                           .then_inc(k["q_ready"], 1)
                        act.wait_ge(k["k_made"], new.i + 1)
                        if due(BT * new.i):
                            act.wait_ge(k["s_made"], BT * new.i)
                        act.activation(KT, bank[5][:, :], ACT.Identity, bias=bk_s[:, :]).then_inc(k["k_ready"], 1)
                    if old.live:
                        act_copy_xt(act, old, NB)
                    if c.live:
                        act.wait_ge(k["av_made"], 4 * (c.i + 1))
                        if due(c.i):
                            act.wait_ge(k["proj_made"], c.i)
                        act.activation(OT, bank[2][:, :], ACT.Copy).then_inc(k["ot_ready"], 1)
                    if out.live:
                        act_payload(act, out, NB)
                rolled(act, NB, 1, 4, body)

            @block.tensor
            def _(pe):
                def score(b, a):
                    if a == 0:
                        pe.wait_ge(k["q_ready"], b.i + 1)
                        pe.wait_ge(k["k_ready"], b.i + 1)
                    if due(BT * b.i + (a - 1)):
                        pe.wait_ge(k["probs_ready"], BT * b.i + (a - 1))
                    pe.matmul(bank[4 + a % 2][:, :], QT[:, a * P:(a + 1) * P], KT,
                              start=True, stop=True).then_inc(k["s_made"], 1)

                def turn(c, g):
                    name = ("even", "odd")[g % 2]
                    if g == 0:
                        pe.wait_ge(k["scaled"], BT * (c.i + 1))
                    if due(2 * c.i + g // 2):
                        pe.wait_ge(k["c_" + name], 2 * c.i + g // 2)
                    for a in range(BT):
                        mm = pe.transpose(chunk(bank[6 + g % 2], a), big[:, c.buf, a, g * P:(g + 1) * P],
                                          ident[:, :])
                    mm.then_inc(k["t_" + name], 1)

                def times_values(c, g):
                    name = ("even", "odd")[g % 2]
                    if g == 0:
                        pe.wait_ge(k["v_ready"], c.i + 1)
                        if due(c.i):
                            pe.wait_ge(k["ot_ready"], c.i)
                    pe.wait_ge(k["c_" + name], 2 * c.i + (g // 2 + 1))
                    pe.matmul(bank[2][:, :], V[:, c.buf, g, :], PT[:, g % 2, :], start=(g == 0),
                              stop=(g == G - 1)).then_inc(k["av_made"], 1)

                def body(at):
                    new, b, c, old, out = at(1), at(0), at(-1), at(-3), at(-4)
                    if b.live:
                        score(b, 2)
                    if c.live:
                        turn(c, 0)
                        turn(c, 1)
                    if b.live:
                        score(b, 3)
                    if new.live:
                        pe.wait_ge(k["a_normed"], new.i + 1)
                        if due(new.i):
                            pe.wait_ge(k["v_ready"], new.i)
                        for j in range(BT):
                            mm = pe.transpose(chunk(bank[0], j), AN[:, j, :], ident[:, :])
                        mm.then_inc(k["a_turned"], 1)
                    if out.live:
                        pe_rank(pe, out, NB)
                    if c.live:
                        times_values(c, 0)
                        turn(c, 2)
                        times_values(c, 1)
                        turn(c, 3)
                    if old.live:
                        pe_route(pe, old, NB)
                    if new.live:
                        pe.wait_ge(k["a_copied"], new.i + 1)
                        if due(BT * new.i - 1):
                            pe.wait_ge(k["probs_ready"], BT * new.i - 1)
                        pe.matmul(bank[4][:, :], WT4[:, 0, :], AXT, start=True, stop=True)\
                          .then_inc(k["q_made"], 1)
                        if due(BT * new.i):
                            pe.wait_ge(k["probs_ready"], BT * new.i)
                        pe.matmul(bank[5][:, :], WT4[:, 1, :], AXT, start=True, stop=True)\
                          .then_inc(k["k_made"], 1)
                    if c.live:
                        times_values(c, 2)
                    if c.live:
                        times_values(c, 3)
                    if old.live:
                        pe_score(pe, old, NB)
                    if new.live:
                        score(new, 0)
                        score(new, 1)
                        for j in range(BT):
                            pe.matmul(chunk(bank[0], j), AXT[:, j * P:(j + 1) * P], WT4[:, 2, :],
                                      start=True, stop=False)
                            mm = pe.matmul(chunk(bank[0], j), one_row[:, :], bias_row[:, 0, :], start=False, stop=True)
                        mm.then_inc(k["v_made"], 1)
                    if c.live:
                        pe.wait_ge(k["ot_ready"], c.i + 1)
                        pe.wait_ge(k["xt_copied"], NB + c.i - 1 if not isinstance(c.i, int) else NB + max(c.i - 1, 0))
                        for j in range(BT):
                            pe.matmul(chunk(bank[3], j), OT[:, j * P:(j + 1) * P], WT4[:, 3, :], start=True, stop=False)
                            mm = pe.matmul(chunk(bank[3], j), one_row[:, :], bias_row[:, 1, :], start=False, stop=True)
                        mm.then_inc(k["proj_made"], 1)
                rolled(pe, NB, 1, 4, body)

            @block.gpsimd
            def _(pool):
                def body(at):
                    ahead, old, out = at(2), at(-3), at(-4)
                    if ahead.live:
                        pool.wait_ge(y_loaded[ahead.buf], 32 * (ahead.uses + 1))
                        pool.tensor_tensor(Y2[:, ahead.buf, 0, :, :], Y2[:, ahead.buf, 0, :, :],
                                           Y2[:, ahead.buf, 1, :, :], ALU.add).then_inc(k["summed"], 1)
                    if out.live:
                        pool_scatter(pool, out, NB)
                    if old.live:
                        pool.wait_ge(k["xt_copied"], NB + old.i + 1)
                        pool.tensor_copy(cut(XTR, W * old.i, W), XT32[:, old.buf, :]).then_inc(k["xt_split"], 1)
                rolled(pool, NB, 2, 4, body)
                for s in scattered:
                    pool.wait_ge(s, BT * TOPK * 16 * NB)

        experts(NT)

        with nc.Block() as block:
            @block.sync
            def _(sp):
                rolled(sp, NB, 0, 0, lambda at: load_y(sp, at(0), NB))

            @block.tensor
            def _(pe):
                def body(at):
                    new, b = at(1), at(0)
                    if new.live:
                        pe_shared_up(pe, new, NB)
                    if b.live:
                        pe_shared_down(pe, b, NB)
                rolled(pe, NB, 1, 0, body)

            @block.scalar
            def _(act):
                def body(at):
                    new, b = at(1), at(0)
                    if new.live:
                        act_shared(act, new, NB)
                    if b.live:
                        act.wait_ge(k["combined"], NB + b.i + 1)
                        act.dma_start(out_t[:, BT * b.i:BT * b.i + BT, :] if isinstance(b.i, int)
                                      else out_t[:, ds(BT * b.i, BT), :], x_block(b)).then_inc(stored[b.buf], 16)
                        act.wait_ge(stored[b.buf], 16 * (b.uses + 1))
                rolled(act, NB, 1, 0, body)

            @block.vector
            def _(dve):
                st = Steps(dve, vec, vec_at[0])
                def body(at):
                    new, b, nxt = at(1), at(0), at(2)
                    if nxt.live:
                        dve_split_kept(dve, st, nxt)
                    if new.live:
                        dve_shared_mul(dve, st, new, NB)
                    if b.live:
                        dve_shared_add(dve, st, b, NB)
                        dve.wait_ge(y_loaded[b.buf], 32 * (NB // 2 + b.uses + 1))
                        st.settle()
                        st.did(dve.tensor_tensor(x_block(b), x_block(b), Y2[:, b.buf, 0, :, :], ALU.add))
                        st.settle()
                        st.signals(dve.tensor_tensor(x_block(b), x_block(b), Y2[:, b.buf, 1, :, :], ALU.add), k["combined"], NB + b.i + 1)
                rolled(dve, NB, 2, 0, body, st, 2 * 2)


_INS = ["L0_attn_batch", "L0_attn_Wq", "L0_attn_bq", "L0_attn_Wk", "L0_attn_bk", "L0_attn_Wv", "L0_attn_bv",
        "L0_attn_Wo", "L0_attn_bo", "L0_ffn_router_DE", "L0_ffn_w_in_shared_FD", "L0_ffn_w_out_shared_DF",
        "L0_ffn_w_swiglu_FD", "L0_ffn_w_in_eDF", "L0_ffn_w_swiglu_eDF", "L0_ffn_w_out_eFD"]


def kernel(**inputs):
    import numpy as np
    import concourse.bacc as bacc
    from concourse.bass_utils import run_bass_kernel_spmd as run

    nc = bacc.Bacc("TRN2", target_bir_lowering=False, num_devices=1)
    arrays, args = {}, []
    for name in _INS:
        a = np.ascontiguousarray(inputs[name])
        arrays[name] = a
        args.append(nc.dram_tensor(name, a.shape, mybir.dt.from_np(a.dtype), kind="ExternalInput").ap())
    shape = arrays["L0_attn_batch"].shape
    args.append(nc.dram_tensor("out", shape, F32, kind="ExternalOutput").ap())
    macaron(nc, *args)
    r = run(nc, [arrays], core_ids=[0])
    return r.results[0]["out"]
```

```python
from contextlib import ExitStack

import concourse.bass as bass
from concourse import mybir

F32 = mybir.dt.float32
F32R = mybir.dt.float32r
BF16 = mybir.dt.bfloat16
I32 = mybir.dt.int32
U32 = mybir.dt.uint32
ACT = mybir.ActivationFunctionType
ALU = mybir.AluOpType
AXX = mybir.AxisListType.X

P = 128
BT = 4
TOPK = 2
EPS = 1e-5
ds = bass.ds


class Steps:

    def __init__(self, eng, sem, n=0):
        self.eng, self.sem, self.base, self.n, self.last = eng, sem, 0, n, None

    def did(self, ins):
        ins.then_inc(self.sem, 1)
        self.n += 1
        self.last = None
        return ins

    def signals(self, ins, sem, count):
        ins.then_inc(sem, 1)
        self.last = sem, count

    def mark(self):
        return self.last or (self.sem, self.base + self.n)

    def settle(self):
        self.eng.wait_ge(*self.mark())

    def enter(self, turn, per_turn):
        self.before = self.base + self.n
        self.base, self.n = self.before + turn * per_turn, 0

    def leave(self, turns, per_turn):
        assert self.n == per_turn, f"steps in a turn of the loop: {self.n}, not {per_turn}"
        self.base, self.n = self.before + turns * per_turn, 0


class At:

    def __init__(self, i, buf, uses, total):
        self.i, self.buf, self.uses = i, buf, uses
        self.live = not isinstance(i, int) or 0 <= i < total


def rolled(eng, total, ahead, behind, body, steps=None, per_turn=0, n=2, peel=2):
    first = -(-(behind + peel) // n) * n
    turns = (total - ahead - first) // n

    def peeled(i):
        body(lambda k: At(i + k, (i + k) % n, (i + k) // n, total))

    for i in range(-ahead, first):
        peeled(i)
    with eng.Fori(0, turns) as r:
        if steps:
            steps.enter(r, per_turn)
        for u in range(n):
            body(lambda k: At(first + r * n + (u + k), (first + u + k) % n, r + (first + u + k) // n, total))
        if steps:
            steps.leave(turns, per_turn)
    for i in range(first + turns * n, total + behind):
        peeled(i)


def due(count):
    return not isinstance(count, int) or count > 0


def macaron(nc, batch, wq, bq, wk, bk, wv, bv, wo, bo, router, w_in_sh, w_out_sh, w_sw_sh,
            w_in_e, w_sw_e, w_out_e, out):
    B, S, D = batch.shape
    E, _, F = w_in_e.shape
    N = B * S
    T = N // P
    NB = T // BT
    W = BT * P
    G = S // P
    FC = F // P
    assert D == P and S == W and FC == 2 and E == 8
    CAP = N + P
    SLOTS = 8
    NT = -(-(TOPK * T + E - 1) // SLOTS) * SLOTS
    PARTS = 4
    SPAN = 2 * SLOTS
    DUMMY = 8
    assert NT - TOPK * T <= DUMMY
    ROW = D + 1
    PADS = TOPK * N
    SCALE = float(D) ** -0.5

    x_t = batch.rearrange("b (j p) d -> p (b j) d", p=P)
    out_t = out.rearrange("b (j p) d -> p (b j) d", p=P)
    pairs = nc.dram_tensor("pairs", [E * CAP + DUMMY * P, ROW], F32).ap()
    results = nc.dram_tensor("results", [PADS + (E + DUMMY) * P, D], F32).ap()
    results_t = results[0:PADS, :].rearrange("(k t p) d -> p k t d", k=TOPK, p=P)

    with ExitStack() as ctx:
        def sb(name, shape, dt=F32):
            return ctx.enter_context(nc.sbuf_tensor(name, shape, dt))

        def sem(name):
            return ctx.enter_context(nc.semaphore(name))

        def sems(name, n):
            return [sem(f"{name}{i}") for i in range(n)]

        bank = [ctx.enter_context(nc.psum_tensor(f"bank{i}", [P, 512], F32)) for i in range(8)]

        X = sb("X", [P, T, D])
        XTR = sb("XTR", [P, N])
        XTH = sb("XTH", [P, 2, W], F32R)
        XTL = sb("XTL", [P, 2, W], F32R)
        WEH = sb("WEH", [P, E * 2 * F], F32R)
        WEL = sb("WEL", [P, E * 2 * F], F32R)
        WOE = sb("WOE", [P, E * FC * D])
        SHH = sb("SHH", [P, 2 * F], F32R)
        SHL = sb("SHL", [P, 2 * F], F32R)
        WOS = sb("WOS", [P, FC, D])
        WT4 = sb("WT4", [P, 4, D])
        RT = sb("RT", [P, E])
        bq_s = sb("bq_s", [P, 1])
        bk_s = sb("bk_s", [P, 1])
        bias_row = sb("bias_row", [1, 2, D])
        bias_parts = sb("bias_parts", [1, 2, 2, D], F32R)
        one_row = sb("one_row", [1, P], F32R)
        ident = sb("ident", [P, P])
        before = sb("before", [P, P], BF16)
        ones = sb("ones", [P, P], BF16)
        expert_no = sb("expert_no", [P, E])
        region = sb("region", [P, E])
        dest = sb("dest", [P, TOPK, T], I32)
        pad_rows = sb("pad_rows", [P, E, ROW])
        pad_at = sb("pad_at", [1, E], I32)
        next_row = sb("next_row", [P, E])
        eps_c = sb("eps_c", [P, 1])
        ints = sb("ints", [P, E * 2], I32)
        tile_no = sb("tile_no", [1, NT])
        upto = sb("upto", [1, E, E])
        tile_i = sb("tile_i", [1, NT], I32)
        expert_of = sb("expert_of", [1, NT], I32)
        row_of = sb("row_of", [1, NT], I32)
        tcnt = sb("tcnt", [1, 4, E])
        tcnt_i = sb("tcnt_i", [1, 2, E], I32)
        tee = sb("tee", [1, E, E])
        tot_t = sb("tot_t", [1, 3, NT])
        XN = sb("XN", [P, 2, BT, D])
        XT32 = sb("XT32", [P, 2, W])
        ST = sb("ST", [P, 2, BT, 6])
        MV = sb("MV", [P, 2, BT, 2])
        SD = sb("SD", [P, 2, BT])
        RST = sb("RST", [P, 2, BT])
        SC = sb("SC", [P, BT, E])
        TOP = sb("TOP", [P, 2, BT, 8])
        TOPI = sb("TOPI", [P, BT, 8], U32)
        TNH = sb("TNH", [P, 2, BT, TOPK])
        GATE = sb("GATE", [P, 2, BT, TOPK])
        HOT = sb("HOT", [P, BT, TOPK, E])
        HOTB = sb("HOTB", [P, BT, E], BF16)
        RANK = sb("RANK", [P, BT, E])
        PICK = sb("PICK", [P, BT, TOPK, E])
        POS = sb("POS", [P, 2, BT, TOPK], U32)
        PAY = sb("PAY", [P, 2, TOPK, BT, ROW])
        arena = sb("arena", [P, 3584])

        def view(at, *shape):
            size = 1
            for n in shape:
                size *= n
            v = arena[:, at:at + size]
            if len(shape) == 1:
                return v
            names = "abc"[:len(shape)]
            return v.rearrange(f"p ({' '.join(names)}) -> p {' '.join(names)}", **dict(zip(names, shape)))

        XS = view(0, SLOTS, ROW)
        YO = view(SLOTS * ROW, SLOTS, D)
        SSG = view(0, FC, W)
        SHH_T = view(FC * W, 2, FC * W)
        AN = view(0, BT, D)
        AXT = view(512, W)
        QT = view(1024, W)
        KT = view(1536, W)
        PT = view(2048, 2, W)
        OT = view(3072, W)
        SHT = view(2048, 2 * F)
        XSH = sb("XSH", [P, 2, P], F32R)
        XSL = sb("XSL", [P, 2, P], F32R)
        SG = sb("SG", [P, 2, F])
        H = sb("H", [P, 2, F])
        HT = sb("HT", [P, 2, F])
        Y2 = sb("Y2", [P, 2, TOPK, BT, D])
        big = sb("big", [P, 2, BT, W])
        V = sb("V", [P, 2, G, D])
        NM = sb("NM", [P, 2, BT, G])
        SUM = sb("SUM", [P, 2, BT, G])
        R1 = sb("R1", [P, BT, G])
        R2 = sb("R2", [P, BT, G])
        R3 = sb("R3", [P, BT, 1])
        R4 = sb("R4", [P, BT, 1])

        vec = sem("vector_steps")
        act_s = sem("scalar_steps")
        pool_s = sem("pool_steps")
        k = dict((n, sem(n)) for n in (
            "weights_loaded small_loaded prep_transposed consts table_done pads_written "
            "normed xt_turned xt_copied xt_split scored topped tanh_done picked ranked "
            "rank_read gate_done pay0 pay1 placed up0 up1 silu0 silu1 hid0 hid1 down shared_added "
            "xs_turned xs_high xs_low e_up e_silu e_hid e_turned e_copied e_down e_out "
            "a_stats a_std a_normed a_turned a_copied q_made k_made v_made q_ready k_ready v_ready "
            "s_made m_ready probs_ready scaled t_even t_odd c_even c_odd av_made ot_ready proj_made updated "
            "carried_s carried_y kept_split r_stats r_std combined padded summed weights_high xt_high").split())
        x_loaded = sems("x_loaded", 2)
        y_loaded = sems("y_loaded", 2)
        scattered = sems("scattered", 2)
        xs_loaded = sems("xs_loaded", SLOTS)
        y_sent = sems("y_sent", SLOTS)
        stored = sems("stored", 2)

        def carry(dve, word=0):
            dve.memset(spare_v[:, word:word + 1], 0.0)

        def pool_carry(pool, which, n):
            if due(n):
                pool.wait_ge(k[which], n)
            word = spare_p[:, 0:1] if which == "carried_s" else spare_p[:, 1:2]
            pool.tensor_tensor(word, spare_p[:, 2:3], spare_p[:, 2:3], ALU.add).then_inc(k[which], 1)

        def x_block(b):
            return X[:, ds(BT * b.i, BT), :] if not isinstance(b.i, int) else X[:, BT * b.i:BT * b.i + BT, :]

        def cut(buf, at, size):
            return buf[:, at:at + size] if isinstance(at, int) else buf[:, ds(at, size)]

        def tile_of(buf, t):
            return buf[:, t:t + 1, :] if isinstance(t, int) else buf[:, ds(t, 1), :]

        def chunk(ap, j):
            return ap[:, j * P:(j + 1) * P]

        wst = view(0, 6, D)
        spare_v = sb("spare_v", [1, 5])
        spare_p = sb("spare_p", [1, 3])
        spare_a = sb("spare_a", [P, 1])
        vec_at = []
        stage = big[:, :, :, :].rearrange("p a b w -> p (a b w)")

        with nc.Block() as block:
            @block.sync
            def _(sp):
                for b in range(2):
                    sp.dma_start(X[:, BT * b:BT * b + BT, :], x_t[:, BT * b:BT * b + BT, :]).then_inc(x_loaded[b], 16)
                sp.wait_ge(k["consts"], 1)
                sp.dma_start(pairs[E * CAP:E * CAP + DUMMY * P, :].rearrange("(e p) r -> p e r", p=P),
                             pad_rows[:, :, :]).then_inc(k["pads_written"], 16)
                sp.wait_ge(k["small_loaded"], 12 * 16)
                st3 = stage.rearrange("p (e g f) -> p e g f", e=E, g=2)
                sp.dma_start(st3[:, :, 0, :], w_in_e.rearrange("e d f -> d e f")).then_inc(k["weights_loaded"], 16)
                sp.dma_start(st3[:, :, 1, :], w_sw_e.rearrange("e d f -> d e f")).then_inc(k["weights_loaded"], 16)
                sp.dma_start(WOE[:, :].rearrange("p (e c d) -> p e c d", e=E, c=FC),
                             w_out_e.rearrange("e (c p) d -> p e c d", p=P)).then_inc(k["weights_loaded"], 16)
                sp.wait_ge(k["pads_written"], 16)

            @block.scalar
            def _(act):
                small = k["small_loaded"]
                act.dma_start(wst[:, 0:2, :],
                              w_in_sh.rearrange("(c p) d -> p c d", p=P)).then_inc(small, 16)
                act.dma_start(wst[:, 2:4, :], w_sw_sh.rearrange("(c p) d -> p c d", p=P)).then_inc(small, 16)
                act.dma_start(wst[:, 4:6, :].rearrange("p c d -> p (c d)"), w_out_sh).then_inc(small, 16)
                for n, w in enumerate((wq, wk, wv, wo)):
                    act.dma_start(XN[:, 0, n, :], w).then_inc(small, 16)
                act.dma_start(RT[:, :], router).then_inc(small, 16)
                act.dma_start(bq_s[:, :], bq.rearrange("(d a) -> d a", a=1)).then_inc(small, 16)
                act.dma_start(bk_s[:, :], bk.rearrange("(d a) -> d a", a=1)).then_inc(small, 16)
                act.dma_start(bias_row[:, 0, :], bv.rearrange("(a d) -> a d", a=1)).then_inc(small, 16)
                act.dma_start(bias_row[:, 1, :], bo.rearrange("(a d) -> a d", a=1)).then_inc(small, 16)
                act.wait_ge(small, 12 * 16)
                act.activation(bq_s[:, :], bq_s[:, :], ACT.Copy, scale=SCALE).then_inc(act_s, 1)

            @block.gpsimd
            def _(pool):
                st = Steps(pool, pool_s)
                for m, v in ((ident, 0.0), (before, 1.0), (ones, 1.0), (eps_c, EPS), (spare_p, 0.0), (pad_rows, 0.0),
                             (upto, 1.0)):
                    st.did(pool.memset(m[tuple(slice(None) for _ in m.shape)], v))
                st.did(pool.iota(ints[:, 0:E], pattern=[[P, E]], base=PADS + E * P, channel_multiplier=1))
                st.settle()
                st.did(pool.affine_select(out=ident[:, :], in_=ident[:, :], compare_op=ALU.not_equal, fill=1.0,
                                          base=0, pattern=[[-1, P]], channel_multiplier=1))
                st.did(pool.affine_select(out=before[:, :], in_=before[:, :], compare_op=ALU.is_gt, fill=0.0,
                                          base=0, pattern=[[1, P]], channel_multiplier=-1))
                st.did(pool.affine_select(out=upto[:, :, :], in_=upto[:, :, :], compare_op=ALU.is_ge, fill=0.0,
                                          base=0, pattern=[[1, E], [-1, E]], channel_multiplier=0))
                pool.tensor_copy(pad_rows[:, :, D:D + 1].bitcast(I32), ints[:, 0:E].unsqueeze(2)).then_inc(k["consts"], 1)
                st.did(pool.iota(dest[:, :, :], pattern=[[N, TOPK], [P, T]], base=0, channel_multiplier=1))
                st.did(pool.iota(tile_i[:, :], pattern=[[1, NT]], base=0, channel_multiplier=0))
                st.did(pool.iota(ints[:, E:2 * E], pattern=[[1, E]], base=0, channel_multiplier=0))
                st.settle()
                st.did(pool.tensor_copy(tile_no[:, :], tile_i[:, :]))
                st.did(pool.tensor_copy(expert_no[:, :], ints[:, E:2 * E]))
                pool.wait_ge(k["consts"], 1)
                st.settle()
                st.did(pool.iota(ints[:, 0:E], pattern=[[CAP, E]], base=0, channel_multiplier=0))
                st.settle()
                st.did(pool.tensor_copy(region[:, :], ints[:, 0:E]))
                st.did(pool.tensor_copy(next_row[:, :], ints[:, 0:E]))
                st.settle()
                pool.wait_ge(k["pads_written"], 16)
                st.did(pool.iota(ints[:, 0:E], pattern=[[P, E]], base=PADS, channel_multiplier=1))
                st.settle()
                st.did(pool.tensor_copy(pad_rows[:, :, D:D + 1].bitcast(I32), ints[:, 0:E].unsqueeze(2)))
                st.settle()

            @block.tensor
            def _(pe):
                pe.wait_ge(k["small_loaded"], 12 * 16)
                pe.wait_ge(pool_s, 12)
                for c in range(4):
                    pe.transpose(chunk(bank[0], c), wst[:, c, :], ident[:, :])
                for n in range(4):
                    pe.transpose(chunk(bank[1], n), XN[:, 0, n, :], ident[:, :])
                for c in range(FC):
                    mm = pe.transpose(chunk(bank[2], c), wst[:, 4 + c, :], ident[:, :])
                mm.then_inc(k["prep_transposed"], 1)

            @block.vector
            def _(dve):
                st = Steps(dve, vec)
                dve.wait_ge(k["prep_transposed"], 1)
                st.did(dve.tensor_copy(SHT, bank[0][:, :]))
                st.did(dve.tensor_copy(WT4[:, :, :].rearrange("p n d -> p (n d)"), bank[1][:, :]))
                st.did(dve.tensor_copy(WOS[:, :, :].rearrange("p n d -> p (n d)"), bank[2][:, 0:F]))
                st.settle()
                st.did(dve.tensor_copy(SHH[:, :], SHT))
                dve.wait_ge(pool_s, 12)
                st.did(dve.tensor_copy(one_row[:, :], ones[0:1, :]))
                st.did(dve.tensor_copy(bias_parts[:, 0, :, :], bias_row[:, :, :]))
                st.settle()
                st.did(dve.tensor_tensor(bias_parts[:, 1, :, :], bias_row[:, :, :],
                                         bias_parts[:, 0, :, :].bitcast(F32), ALU.subtract))
                st.did(dve.tensor_tensor(SHL[:, :], SHT, SHH[:, :].bitcast(F32), ALU.subtract))
                st.settle()
                vec_at.append(st.n)

        def dve_table(dve, st, ffn):
            st.settle()
            st.did(dve.tensor_copy(pad_at[:, :], next_row[0:1, :]))
            cnt, tiles, ends = tcnt[:, 0, :], tcnt[:, 1, :], tcnt[:, 2, :]
            st.did(dve.tensor_tensor(cnt, next_row[0:1, :], region[0:1, :], ALU.subtract))
            st.settle()
            st.did(dve.tensor_scalar(tcnt_i[:, 0, :], cnt, float(P - 1), None, ALU.add))
            st.settle()
            st.did(dve.tensor_scalar(tcnt_i[:, 1, :], tcnt_i[:, 0, :], 7, None, ALU.arith_shift_right))
            st.settle()
            st.did(dve.tensor_copy(tiles, tcnt_i[:, 1, :]))
            st.settle()
            st.did(dve.tensor_tensor(tee[:, :, :], upto[:, :, :], tiles.unsqueeze(1).to_broadcast([1, E, E]), ALU.mult))
            st.settle()
            st.did(dve.tensor_reduce(ends, tee[:, :, :], AXX, ALU.add))
            st.settle()
            tbl = big[0:1, 0, :, :].rearrange("p a w -> p (a w)")[:, 0:NT * E].rearrange("p (t e) -> p t e", e=E)
            st.did(dve.tensor_tensor(tbl, tile_no[:, :].unsqueeze(2).to_broadcast([1, NT, E]),
                                     ends.unsqueeze(1).to_broadcast([1, NT, E]), ALU.is_ge))
            st.settle()
            ex, gone, row = tot_t[:, 0, :], tot_t[:, 1, :], tot_t[:, 2, :]
            st.did(dve.tensor_reduce(ex, tbl, AXX, ALU.add))
            st.settle()
            st.did(dve.tensor_tensor(tbl, tbl, tiles.unsqueeze(1).to_broadcast([1, NT, E]), ALU.mult))
            st.settle()
            st.did(dve.tensor_reduce(gone, tbl, AXX, ALU.add))
            st.did(dve.tensor_scalar(expert_of[:, :], ex, float(E - 1), None, ALU.min))
            st.settle()
            st.did(dve.tensor_tensor(row, tile_no[:, :], gone, ALU.subtract))
            st.did(dve.tensor_scalar(ex, ex, float(CAP), None, ALU.mult))
            st.settle()
            st.did(dve.scalar_tensor_tensor(out=row_of[:, :], in0=row, scalar=float(P), in1=ex,
                                            op0=ALU.mult, op1=ALU.add))
            st.signals(dve.tensor_copy(next_row[:, :], region[:, :]), k["table_done"], ffn + 1)
            st.settle()

        def sp_pad(sp, ffn):
            sp.wait_ge(k["table_done"], ffn + 1)
            pads = [sp.alloc_register(f"pad{ffn}_{e}") for e in range(E)]
            sp.reg_load(pads, pad_at[0:1, :])
            for e in range(E):
                row = sp.snap(pads[e], min_val=e * CAP, max_val=e * CAP + N)
                sp.dma_start(pairs[ds(row, P), :], pad_rows[:, e, :]).then_inc(k["padded"], 16)
            sp.wait_ge(k["padded"], 16 * E * (ffn + 1))

        def xt_bank(done):
            return bank[3 if done else 0]

        def score_bank(done):
            return bank[1 if done else 7]

        def pe_route(pe, b, done):
            n = done + b.i
            pe.wait_ge(k["normed"], n + 1)
            for j in range(BT):
                mm = pe.transpose(chunk(xt_bank(done), j), XN[:, b.buf, j, :], ident[:, :])
            mm.then_inc(k["xt_turned"], 1)

        def pe_score(pe, b, done):
            n = done + b.i
            pe.wait_ge(k["xt_copied"], n + 1)
            if done and due(n):
                pe.wait_ge(k["rank_read"], n)
            for j in range(BT):
                mm = pe.matmul(score_bank(done)[:, j * E:(j + 1) * E], XT32[:, b.buf, j * P:(j + 1) * P], RT[:, :],
                               start=True, stop=True)
            mm.then_inc(k["scored"], 1)

        def pe_rank(pe, b, done):
            pe.wait_ge(k["picked"], done + b.i + 1)
            rk = bank[1][:, 0:BT * E]
            hot = HOTB[:, :, :].rearrange("p j e -> p (j e)")
            pe.matmul(rk, before[:, :], hot, start=True, stop=False)
            for s in range(1, BT):
                pe.matmul(rk[:, s * E:], ones[:, :], hot[:, 0:(BT - s) * E], start=False, stop=(s == BT - 1))
            tot = bank[1][:, BT * E:(BT + 1) * E]
            for j in range(BT):
                mm = pe.matmul(tot, ones[:, :], hot[:, j * E:(j + 1) * E], start=(j == 0), stop=(j == BT - 1))
            mm.then_inc(k["ranked"], 1)

        def act_copy_xt(act, b, done):
            n = done + b.i
            act.wait_ge(k["xt_turned"], n + 1)
            if done:
                act.wait_ge(k["xt_split"], n - 1)
            act.activation(XT32[:, b.buf, :], xt_bank(done)[:, :], ACT.Copy).then_inc(k["xt_copied"], 1)

        def act_gates(act, b, done):
            n = done + b.i
            act.wait_ge(k["topped"], n + 1)
            act.activation(TNH[:, b.buf, :, :], TOP[:, b.buf, :, 0:TOPK], ACT.Tanh, scale=0.5)\
               .then_inc(k["tanh_done"], 1)

        def act_payload(act, b, done):
            n = done + b.i
            act.wait_ge(k["gate_done"], n + 1)
            if due(BT * TOPK * 16 * (done // 2 + b.uses)):
                act.wait_ge(scattered[b.buf], BT * TOPK * 16 * (done // 2 + b.uses))
            for j in range(BT):
                ins = act.activation(PAY[:, b.buf, 1, j, 0:D], XN[:, b.buf, j, :], ACT.Copy,
                                     scale=GATE[:, b.buf, j, 1:2])
            ins.then_inc(k["pay1"], 1)

        def dve_moments(dve, st, b, which, sem_, count):
            dve.wait_ge(sem_, count)
            carry(dve, 1 + which)
            for j in range(BT):
                st.did(dve.bn_stats(ST[:, which, j, :], tile_of(X, BT * b.i + j).rearrange("p a d -> p (a d)")))
            return st.mark()

        def dve_mean_var(dve, st, b, which, after, name, done):
            dve.wait_ge(*after)
            carry(dve, 3 + which)
            for j in range(BT):
                ins = dve.bn_aggr(MV[:, which, j, :], ST[:, which, j, :])
            st.signals(ins, k[name], done + b.i + 1)

        def act_std(act, b, which, stats, name, done):
            act.wait_ge(k[stats], done + b.i + 1)
            act.activation(SD[:, which, :], MV[:, which, :, 1], ACT.Sqrt, bias=eps_c[:, :]).then_inc(k[name], 1)

        def dve_rstd(dve, st, b, which, name, done):
            dve.wait_ge(k[name], done + b.i + 1)
            st.did(dve.reciprocal(RST[:, which, :], SD[:, which, :]))
            return st.mark()

        def dve_norm(dve, st, b, done):
            n = done + b.i
            if done:
                dve.wait_ge(k["pay1"], n - 1)
            for j in range(BT):
                t = BT * b.i + j
                ins = dve.tensor_scalar(XN[:, b.buf, j:j + 1, :], tile_of(X, t), MV[:, 1, j, 0:1],
                                        RST[:, 1, j:j + 1], ALU.subtract, ALU.mult)
            st.signals(ins, k["normed"], n + 1)

        def act_high(act, b):
            act.activation(XTH[:, b.buf, :], xt_bank(0)[:, :], ACT.Copy).then_inc(k["xt_high"], 1)

        def dve_low(dve, st, b):
            dve.wait_ge(k["xt_high"], b.i + 1)
            st.signals(dve.tensor_tensor(XTL[:, b.buf, :], XT32[:, b.buf, :], XTH[:, b.buf, :].bitcast(F32),
                                         ALU.subtract), k["xt_split"], b.i + 1)

        def act_high_kept(act, b):
            act.activation(XTH[:, b.buf, :], cut(XTR, W * b.i, W), ACT.Copy).then_inc(k["xt_high"], 1)

        def dve_low_kept(dve, st, b):
            dve.wait_ge(k["xt_high"], NB + b.i + 1)
            st.signals(dve.tensor_tensor(XTL[:, b.buf, :], cut(XTR, W * b.i, W), XTH[:, b.buf, :].bitcast(F32),
                                         ALU.subtract), k["kept_split"], b.i + 1)

        def dve_top(dve, st, b, done):
            n = done + b.i
            dve.wait_ge(k["scored"], n + 1)
            st.did(dve.tensor_copy(SC[:, :, :].rearrange("p j e -> p (j e)"), score_bank(done)[:, 0:BT * E]))
            st.settle()
            carry(dve)
            for j in range(BT):
                ins = dve.max(TOP[:, b.buf, j, :], SC[:, j, :])
            st.signals(ins, k["topped"], n + 1)
            st.settle()
            carry(dve)
            for j in range(BT):
                st.did(dve.max_index(TOPI[:, j, :], TOP[:, b.buf, j, :], SC[:, j, :]))
            st.settle()
            st.did(dve.tensor_tensor(HOT[:, :, :, :],
                                     TOPI[:, :, 0:TOPK].unsqueeze(3).to_broadcast([P, BT, TOPK, E]),
                                     expert_no[:, :].unsqueeze(1).unsqueeze(1).to_broadcast([P, BT, TOPK, E]),
                                     ALU.is_equal))
            st.settle()
            st.signals(dve.tensor_tensor(HOTB[:, :, :], HOT[:, :, 0, :], HOT[:, :, 1, :], ALU.add), k["picked"], n + 1)

        def dve_payload(dve, st, b, done):
            n = done + b.i
            dve.wait_ge(k["tanh_done"], n + 1)
            if due(BT * TOPK * 16 * (done // 2 + b.uses)):
                dve.wait_ge(scattered[b.buf], BT * TOPK * 16 * (done // 2 + b.uses))
            st.signals(dve.tensor_scalar(GATE[:, b.buf, :, :], TNH[:, b.buf, :, :], 0.5, 0.5, ALU.mult, ALU.add), k["gate_done"], n + 1)
            where = dest[:, :, BT * b.i:BT * b.i + BT] if isinstance(b.i, int) else dest[:, :, ds(BT * b.i, BT)]
            st.did(dve.tensor_copy(PAY[:, b.buf, :, :, D:D + 1].bitcast(I32), where.unsqueeze(3)))
            st.settle()
            for j in range(BT):
                ins = dve.tensor_scalar(PAY[:, b.buf, 0, j, 0:D], XN[:, b.buf, j, :],
                                               GATE[:, b.buf, j, 0:1], None, ALU.mult)
            st.signals(ins, k["pay0"], n + 1)

        def dve_place(dve, st, b, done):
            dve.wait_ge(k["ranked"], done + b.i + 1)
            st.did(dve.tensor_tensor(RANK[:, :, :], bank[1][:, 0:BT * E].rearrange("p (j e) -> p j e", e=E),
                                     next_row[:, :].unsqueeze(1).to_broadcast([P, BT, E]), ALU.add))
            st.settle()
            st.signals(dve.tensor_tensor(next_row[:, :], bank[1][:, BT * E:(BT + 1) * E], next_row[:, :], ALU.add), k["rank_read"], done + b.i + 1)
            st.did(dve.tensor_tensor(PICK[:, :, :, :], HOT[:, :, :, :],
                                     RANK[:, :, :].unsqueeze(2).to_broadcast([P, BT, TOPK, E]), ALU.mult))
            st.settle()
            with nc.allow_low_precision(reason="row numbers: whole, below 2^24"):
                st.signals(dve.tensor_reduce(POS[:, b.buf, :, :], PICK[:, :, :, :], AXX, ALU.add), k["placed"], done + b.i + 1)

        def pool_scatter(pool, b, done):
            n = done + b.i
            pool.wait_ge(k["pay0"], n + 1)
            pool.wait_ge(k["pay1"], n + 1)
            pool.wait_ge(k["placed"], n + 1)
            pool_carry(pool, "carried_s", n)
            for j in range(BT):
                for c in range(TOPK):
                    pool.indirect_dma_start(pairs, bass.IndirectOffsetOnAxis(ap=POS[:, b.buf, j, c:c + 1], axis=0),
                                            PAY[:, b.buf, c, j, :], None).then_inc(scattered[b.buf], 16)

        def pe_shared_up(pe, b, done):
            n = done + b.i
            pe.wait_ge(k["xt_split" if done == 0 else "kept_split"], b.i + 1)
            hi, lo = XTH[:, b.buf, :], XTL[:, b.buf, :]
            for c in range(FC):
                if due(n):
                    pe.wait_ge(k[f"hid{c}"], n)
                for g in range(2):
                    ps = bank[2 + 2 * c + g]
                    w = slice(g * F + c * P, g * F + (c + 1) * P)
                    pe.matmul(ps[:, :], SHL[:, w], hi, start=True, stop=False)
                    pe.matmul(ps[:, :], SHH[:, w], lo, start=False, stop=False)
                    mm = pe.matmul(ps[:, :], SHH[:, w], hi, start=False, stop=True)
                mm.then_inc(k[f"up{c}"], 1)

        def act_shared(act, b, done):
            n = done + b.i
            for c in range(FC):
                act.wait_ge(k[f"up{c}"], n + 1)
                act.activation(SSG[:, c, :], bank[2 + 2 * c][:, :], ACT.Silu).then_inc(k[f"silu{c}"], 1)

        def dve_shared_mul(dve, st, b, done):
            n = done + b.i
            for c in range(FC):
                dve.wait_ge(k[f"silu{c}"], n + 1)
                st.signals(dve.tensor_tensor(SHH_T[:, b.buf, c * W:(c + 1) * W], bank[3 + 2 * c][:, :], SSG[:, c, :], ALU.mult), k[f"hid{c}"], n + 1)

        def pe_shared_down(pe, b, done):
            n = done + b.i
            pe.wait_ge(k["hid1"], n + 1)
            if (done or isinstance(n, int)) and due(n):
                pe.wait_ge(k["shared_added"], n)
            for j in range(BT):
                for c in range(FC):
                    mm = pe.matmul(chunk(bank[6], j), SHH_T[:, b.buf, c * W + j * P:c * W + (j + 1) * P], WOS[:, c, :],
                                   start=(c == 0), stop=(c == FC - 1))
            mm.then_inc(k["down"], 1)

        def dve_shared_add(dve, st, b, done):
            dve.wait_ge(k["down"], done + b.i + 1)
            st.signals(dve.scalar_tensor_tensor(out=x_block(b), in0=bank[6][:, :].rearrange("p (j d) -> p j d", d=D),
                                            scalar=0.5, in1=x_block(b), op0=ALU.mult, op1=ALU.add), k["shared_added"], done + b.i + 1)

        with nc.Block() as block:
            @block.sync
            def _(sp):
                with sp.Fori(1, NB // 2) as r:
                    for u in range(2):
                        sp.wait_ge(x_loaded[u], 16 * r)
                        sp.dma_start(X[:, ds(2 * BT * r + BT * u, BT), :],
                                     x_t[:, ds(2 * BT * r + BT * u, BT), :]).then_inc(x_loaded[u], 16)
                sp_pad(sp, 0)

            @block.vector
            def _(dve):
                st = Steps(dve, vec, vec_at[0])

                def body(at):
                    ahead, new, b, c = at(2), at(1), at(0), at(-1)
                    if new.live:
                        rst = dve_rstd(dve, st, new, 1, "r_std", 0)
                    if new.live:
                        dve.wait_ge(*rst)
                        dve_norm(dve, st, new, 0)
                    if b.live:
                        dve_top(dve, st, b, 0)
                        dve_shared_mul(dve, st, b, 0)
                    if new.live:
                        dve_low(dve, st, new)
                    if ahead.live:
                        seen = dve_moments(dve, st, ahead, 1, x_loaded[ahead.buf], 16 * (ahead.uses + 1))
                    if b.live:
                        dve_payload(dve, st, b, 0)
                    if ahead.live:
                        dve_mean_var(dve, st, ahead, 1, seen, "r_stats", 0)
                    if b.live:
                        dve_place(dve, st, b, 0)
                    if c.live:
                        dve_shared_add(dve, st, c, 0)
                    if isinstance(b.i, int) and 0 <= b.i < PARTS:
                        dve.wait_ge(k["weights_high"], 1)
                        part = slice(b.i * E * 2 * F // PARTS, (b.i + 1) * E * 2 * F // PARTS)
                        st.did(dve.tensor_tensor(WEL[:, part], stage[:, part], WEH[:, part].bitcast(F32),
                                                 ALU.subtract))
                rolled(dve, NB, 2, 1, body, st, 2 * 14)
                dve_table(dve, st, 0)
                vec_at[0] = st.base + st.n

            @block.scalar
            def _(act):
                def body(at):
                    ahead, new, b = at(2), at(1), at(0)
                    if b.live:
                        act_shared(act, b, 0)
                        act_gates(act, b, 0)
                    if new.live:
                        act_copy_xt(act, new, 0)
                        act_high(act, new)
                    if b.live:
                        act_payload(act, b, 0)
                    if ahead.live:
                        act_std(act, ahead, 1, "r_stats", "r_std", 0)
                    act.activation(spare_a[:, :], eps_c[:, :], ACT.Silu)
                    if isinstance(b.i, int) and b.i == -1:
                        act.wait_ge(k["weights_loaded"], 48)
                        act.activation(WEH[:, :], stage, ACT.Copy).then_inc(k["weights_high"], 1)
                rolled(act, NB, 2, 0, body)

            @block.tensor
            def _(pe):
                def body(at):
                    new, b, c = at(1), at(0), at(-1)
                    if b.live:
                        pe_shared_up(pe, b, 0)
                    if new.live:
                        pe_route(pe, new, 0)
                    if c.live:
                        pe_shared_down(pe, c, 0)
                    if b.live:
                        pe_rank(pe, b, 0)
                    if new.live:
                        pe_score(pe, new, 0)
                rolled(pe, NB, 1, 1, body)

            @block.gpsimd
            def _(pool):
                rolled(pool, NB, 0, 0, lambda at: pool_scatter(pool, at(0), 0))
                for s in scattered:
                    pool.wait_ge(s, BT * TOPK * 16 * NB // 2)

        def experts(done):
            first = done == 0
            ffn = 0 if first else 1
            with nc.Block() as block:
                @block.vector
                def _(dve):
                    st = Steps(dve, vec, vec_at[0])
                    def body(at):
                        nx, t, od = at(2), at(0), at(-2)
                        if t.live:
                            dve.wait_ge(k["e_silu"], done + t.i + 1)
                            st.signals(dve.tensor_tensor(H[:, t.buf % 2, :], bank[2 + t.buf % 2][:, F:2 * F],
                                                     SG[:, t.buf % 2, :], ALU.mult), k["e_hid"], done + t.i + 1)
                        if od.live:
                            dve.wait_ge(k["e_down"], done + od.i + 1)
                            if due(16 * (done // SLOTS + od.uses)):
                                dve.wait_ge(y_sent[od.buf], 16 * (done // SLOTS + od.uses))
                            st.signals(dve.tensor_scalar(YO[:, od.buf, :], bank[6 + od.buf % 2][:, 0:D], 0.5, None,
                                                     ALU.mult), k["e_out"], done + od.i + 1)
                        if nx.live:
                            dve.wait_ge(k["xs_high"], done + nx.i + 1)
                            st.signals(dve.tensor_tensor(XSL[:, nx.buf % 2, :], bank[nx.buf % 2][:, 0:P],
                                                     XSH[:, nx.buf % 2, :].bitcast(F32), ALU.subtract), k["xs_low"], done + nx.i + 1)
                    rolled(dve, NT, 2, 2, body, st, 0, n=SLOTS, peel=SLOTS)
                    vec_at[0] = st.base + st.n

                @block.gpsimd
                def _(pool):
                    def send(at):
                        t = at(0)
                        pool.wait_ge(k["e_out"], done + t.i + 1)
                        pool_carry(pool, "carried_y", done + t.i)
                        pool.indirect_dma_start(
                            results, bass.IndirectOffsetOnAxis(ap=XS[:, t.buf, D:D + 1].bitcast(U32), axis=0),
                            YO[:, t.buf, :], None).then_inc(y_sent[t.buf], 16)
                    rolled(pool, NT, 0, 0, send, n=SLOTS)
                    for s in y_sent:
                        pool.wait_ge(s, 16 * (done + NT) // SLOTS)

                @block.sync
                def _(sp):
                    rows = [sp.alloc_register(f"row{ffn}_{i}") for i in range(SLOTS)]
                    def load(r):
                        sp.reg_load(rows, row_of[0:1, ds(r * SLOTS, SLOTS)])
                        for u in range(SLOTS):
                            row = sp.snap(rows[u], min_val=0, max_val=E * CAP + (DUMMY - 1) * P)
                            if due((r + done // SLOTS) * 16):
                                sp.wait_ge(y_sent[u], (r + done // SLOTS) * 16)
                            sp.dma_start(XS[:, u, :], pairs[ds(row, P), :]).then_inc(xs_loaded[u], 16)
                    load(0)
                    with sp.Fori(1, NT // SLOTS) as r:
                        load(r)

                @block.scalar
                def _(act):
                    def body(at):
                        nx, t, ld = at(2), at(0), at(-1)
                        if t.live:
                            act.wait_ge(k["e_up"], done + t.i + 1)
                            act.activation(SG[:, t.buf % 2, :], bank[2 + t.buf % 2][:, 0:F], ACT.Silu)\
                               .then_inc(k["e_silu"], 1)
                        if ld.live:
                            act.wait_ge(k["e_turned"], done + ld.i + 1)
                            act.activation(HT[:, ld.buf % 2, :], bank[4 + ld.buf % 2][:, 0:F], ACT.Copy)\
                               .then_inc(k["e_copied"], 1)
                        if nx.live:
                            act.wait_ge(k["xs_turned"], done + nx.i + 1)
                            act.activation(XSH[:, nx.buf % 2, :], bank[nx.buf % 2][:, 0:P], ACT.Copy)\
                               .then_inc(k["xs_high"], 1)
                    rolled(act, NT, 2, 1, body, n=SLOTS)

                @block.tensor
                def _(pe):
                    pe.wait_ge(k["table_done"], ffn + 1)
                    regs = [pe.alloc_register(f"expert{ffn}_{i}") for i in range(SLOTS + 2)]

                    def expert(reg):
                        return pe.snap(reg, min_val=0, max_val=E - 1)

                    def body(nx, t, ld, od, up_reg, down_reg, wanted=None):
                        if t.live:
                            e = expert(up_reg)
                            ps = bank[2 + t.buf % 2][:, :]
                            hi, lo = XSH[:, t.buf % 2, :], XSL[:, t.buf % 2, :]
                            pe.wait_ge(k["xs_low"], done + t.i + 1)
                            pe.matmul(ps, lo, WEH[:, ds(e * 2 * F, 2 * F)], start=True, stop=False)
                            pe.matmul(ps, hi, WEL[:, ds(e * 2 * F, 2 * F)], start=False, stop=False)
                            pe.matmul(ps, hi, WEH[:, ds(e * 2 * F, 2 * F)], start=False, stop=True)\
                              .then_inc(k["e_up"], 1)
                        if od.live:
                            e = expert(down_reg)
                        if wanted:
                            pe.reg_load(*wanted)
                        if od.live:
                            pe.wait_ge(k["e_copied"], done + od.i + 1)
                            if not t.live:
                                pe.wait_ge(k["e_out"], done + od.i - 1)
                            for c in range(FC):
                                mm = pe.matmul(bank[6 + od.buf % 2][:, 0:D], HT[:, od.buf % 2, c * P:(c + 1) * P],
                                               WOE[:, ds(e * FC * D + c * D, D)], start=(c == 0), stop=(c == FC - 1))
                            mm.then_inc(k["e_down"], 1)
                        if ld.live:
                            pe.wait_ge(k["e_hid"], done + ld.i + 1)
                            for c in range(FC):
                                mm = pe.transpose(chunk(bank[4 + ld.buf % 2], c), H[:, ld.buf % 2, c * P:(c + 1) * P],
                                                  ident[:, :])
                            mm.then_inc(k["e_turned"], 1)
                        if nx.live:
                            pe.wait_ge(xs_loaded[nx.buf], 16 * (done // SLOTS + nx.uses + 1))
                            pe.transpose(bank[nx.buf % 2][:, 0:P], XS[:, nx.buf, 0:D], ident[:, :])\
                              .then_inc(k["xs_turned"], 1)

                    def some(lo, hi):
                        of = range(max(lo - 2, 0), min(hi, NT))
                        pe.reg_load(regs[:len(of)], expert_of[0:1, of[0]:of[-1] + 1])
                        for i in range(lo, hi):
                            def at(d):
                                return At(i + d, (i + d) % SLOTS, (i + d) // SLOTS, NT)
                            body(at(2), at(0), at(-1), at(-2), regs[of.index(i)] if i in of else None,
                                 regs[of.index(i - 2)] if i - 2 in of else None)

                    turns = (NT - 6) // SPAN
                    some(-2, 4)
                    pe.reg_load(regs[:6], expert_of[0:1, 2:8])
                    with pe.Fori(0, turns) as r:
                        for u in range(SPAN):
                            half, v = u // SLOTS, u % SLOTS
                            wanted = None
                            if v == 1:
                                wanted = regs[6:], expert_of[0:1, ds(r * SPAN + half * SLOTS + 8, 4)]
                            if v == 6:
                                wanted = regs[:6], expert_of[0:1, ds(r * SPAN + (half + 1) * SLOTS + 2, 6)]
                            def at(d):
                                return At(r * SPAN + (4 + u + d), (4 + u + d) % SLOTS,
                                          r * (SPAN // SLOTS) + (4 + u + d) // SLOTS, NT)
                            body(at(2), at(0), at(-1), at(-2), regs[v + 2], regs[v], wanted)
                    some(4 + turns * SPAN, NT + 2)

        experts(0)

        def load_y(sp, b, done):
            if due(done + b.i - 1):
                sp.wait_ge(k["combined"], done + b.i - 1)
            src = results_t[:, :, BT * b.i:BT * b.i + BT, :] if isinstance(b.i, int) else results_t[:, :, ds(BT * b.i, BT), :]
            for c in range(TOPK):
                sp.dma_start(Y2[:, b.buf, c, :, :], src[:, c, :, :]).then_inc(y_loaded[b.buf], 8 * 2)

        def pool_sum(pool, b, done):
            pool.wait_ge(y_loaded[b.buf], 32 * (done // 2 + b.uses + 1))
            pool.tensor_tensor(Y2[:, b.buf, 0, :, :], Y2[:, b.buf, 0, :, :], Y2[:, b.buf, 1, :, :], ALU.add)\
                .then_inc(k["summed"], 1)

        def dve_add_results(dve, st, b, done):
            dve.wait_ge(k["summed"], done + b.i + 1)
            st.signals(dve.tensor_tensor(x_block(b), x_block(b), Y2[:, b.buf, 0, :, :], ALU.add),
                       k["combined"], done + b.i + 1)
            return st.mark()

        with nc.Block() as block:
            @block.sync
            def _(sp):
                rolled(sp, NB, 0, 0, lambda at: load_y(sp, at(0), 0))
                sp_pad(sp, 1)

            @block.vector
            def _(dve):
                st = Steps(dve, vec, vec_at[0])

                def maximum(b, a):
                    dve.wait_ge(k["s_made"], BT * b.i + (a + 1))
                    st.signals(dve.tensor_reduce(NM[:, b.buf, a, :],
                                                 bank[4 + a % 2][:, :].rearrange("p (g c) -> p g c", c=P),
                                                 AXX, ALU.max, negate=True), k["m_ready"], BT * b.i + (a + 1))

                def normalise(new):
                    for j in range(BT):
                        ins = dve.tensor_scalar(AN[:, j:j + 1, :], tile_of(X, BT * new.i + j),
                                                MV[:, 0, j, 0:1], RST[:, 0, j:j + 1],
                                                ALU.subtract, ALU.mult)
                    st.signals(ins, k["a_normed"], new.i + 1)

                def update(c):
                    dve.wait_ge(k["proj_made"], c.i + 1)
                    st.signals(dve.tensor_tensor(x_block(c), bank[3][:, :].rearrange("p (j d) -> p j d", d=D),
                                                 x_block(c), ALU.add), k["updated"], c.i + 1)
                    return st.mark()

                def weight(b, n, after):
                    dve.wait_ge(*after)
                    sm = SUM[:, b.buf, :, :]
                    if n == 0:
                        ins = dve.reciprocal(R1[:, :, :], sm)
                    elif n == 1:
                        ins = dve.tensor_tensor(R2[:, :, :], R1[:, :, :], sm, ALU.mult)
                    elif n == 2:
                        ins = dve.tensor_reduce(R3[:, :, :], R2[:, :, :].unsqueeze(2), AXX, ALU.add)
                    elif n == 3:
                        ins = dve.tensor_scalar(R3[:, :, :], R3[:, :, :], 1e-6, None, ALU.add)
                    elif n == 4:
                        ins = dve.reciprocal(R4[:, :, :], R3[:, :, :])
                    else:
                        ins = dve.tensor_tensor(R2[:, :, :], R1[:, :, :], R4[:, :, :].to_broadcast([P, BT, G]),
                                                ALU.mult)
                    st.did(ins)
                    return st.mark()

                def scale(b, a):
                    e3 = big[:, b.buf, a, :].rearrange("p (g c) -> p g c", c=P)
                    st.signals(dve.tensor_tensor(e3, e3, R2[:, a, :].unsqueeze(2).to_broadcast([P, G, P]),
                                                 ALU.mult), k["scaled"], BT * b.i + (a + 1))

                def body(at):
                    ahead, new, b, c, upd, old, out = (at(d) for d in range(2, -5, -1))
                    if b.live:
                        maximum(b, 0)
                        maximum(b, 1)
                    if c.live:
                        st.settle()
                        for a in range(BT):
                            scale(c, a)
                    if new.live:
                        rst_new = dve_rstd(dve, st, new, 0, "a_std", 0)
                    if old.live:
                        rst_old = dve_rstd(dve, st, old, 1, "r_std", NB)
                    if new.live:
                        dve.wait_ge(*rst_new)
                        normalise(new)
                    if b.live:
                        maximum(b, 2)
                    if upd.live:
                        updated = update(upd)
                    if old.live:
                        dve.wait_ge(*rst_old)
                        dve_norm(dve, st, old, NB)
                    if b.live:
                        maximum(b, 3)
                    if out.live:
                        dve_payload(dve, st, out, NB)
                        dve_place(dve, st, out, NB)
                    if ahead.live:
                        added = dve_add_results(dve, st, ahead, 0)
                    if b.live:
                        r1 = weight(b, 0, (k["probs_ready"], BT * (b.i + 1)))
                    if upd.live:
                        seen_u = dve_moments(dve, st, upd, 1, *updated)
                    if b.live:
                        r2 = weight(b, 1, r1)
                    if ahead.live:
                        seen = dve_moments(dve, st, ahead, 0, *added)
                    if b.live:
                        r3 = weight(b, 2, r2)
                    if upd.live:
                        dve_mean_var(dve, st, upd, 1, seen_u, "r_stats", NB)
                    if b.live:
                        r3 = weight(b, 3, r3)
                    if ahead.live:
                        dve_mean_var(dve, st, ahead, 0, seen, "a_stats", 0)
                    if b.live:
                        r4 = weight(b, 4, r3)
                        weight(b, 5, r4)
                    if old.live:
                        dve_top(dve, st, old, NB)
                rolled(dve, NB, 2, 4, body, st, 2 * 25)
                dve_table(dve, st, 1)
                vec_at[0] = st.base + st.n

            @block.scalar
            def _(act):
                def exps(b, a):
                    act.wait_ge(k["m_ready"], BT * b.i + (a + 1))
                    for g in range(G):
                        ins = act.activation(big[:, b.buf, a, g * P:(g + 1) * P], chunk(bank[4 + a % 2], g),
                                             ACT.Exp, bias=NM[:, b.buf, a, g:g + 1],
                                             accum_out=SUM[:, b.buf, a, g:g + 1])
                    ins.then_inc(k["probs_ready"], 1)

                def copy_turned(c, g):
                    h = g // 2
                    if g % 2 == 0:
                        act.wait_ge(k["t_even"], 2 * c.i + (h + 1))
                        act.activation(PT[:, 0, :], bank[6][:, :], ACT.Copy).then_inc(k["c_even"], 1)
                    else:
                        act.wait_ge(k["t_odd"], 2 * c.i + (h + 1))
                        act.activation(PT[:, 1, :], bank[7][:, :], ACT.Copy).then_inc(k["c_odd"], 1)

                def body(at):
                    ahead, new, b, c, upd, old, out = (at(d) for d in range(2, -5, -1))
                    if b.live:
                        exps(b, 0)
                        exps(b, 1)
                        act.wait_ge(k["v_made"], b.i + 1)
                        act.activation(V[:, b.buf, :, :].rearrange("p g d -> p (g d)"), bank[0][:, :], ACT.Copy)\
                           .then_inc(k["v_ready"], 1)
                        exps(b, 2)
                    if c.live:
                        copy_turned(c, 0)
                        copy_turned(c, 1)
                    if b.live:
                        exps(b, 3)
                    if c.live:
                        copy_turned(c, 2)
                    if new.live:
                        act.wait_ge(k["a_turned"], new.i + 1)
                        act.activation(AXT, bank[0][:, :], ACT.Copy).then_inc(k["a_copied"], 1)
                    if c.live:
                        copy_turned(c, 3)
                    if old.live:
                        act_copy_xt(act, old, NB)
                    if new.live:
                        act.wait_ge(k["q_made"], new.i + 1)
                        act.activation(QT, bank[4][:, :], ACT.Identity, bias=bq_s[:, :], scale=SCALE)\
                           .then_inc(k["q_ready"], 1)
                        act.wait_ge(k["k_made"], new.i + 1)
                        act.activation(KT, bank[5][:, :], ACT.Identity, bias=bk_s[:, :]).then_inc(k["k_ready"], 1)
                    if ahead.live:
                        act_std(act, ahead, 0, "a_stats", "a_std", 0)
                    if upd.live:
                        act_std(act, upd, 1, "r_stats", "r_std", NB)
                    if old.live:
                        act_gates(act, old, NB)
                    if c.live:
                        act.wait_ge(k["av_made"], 4 * (c.i + 1))
                        act.activation(OT, bank[2][:, :], ACT.Copy).then_inc(k["ot_ready"], 1)
                rolled(act, NB, 2, 4, body)

            @block.tensor
            def _(pe):
                def pe_bias(ps, n):
                    for part in range(2):
                        pe.matmul(ps[:, :].rearrange("p (j d) -> p j d", d=D), one_row[:, :],
                                  bias_parts[:, part, n:n + 1, :].to_broadcast([1, BT, D]),
                                  start=(part == 0), stop=False)

                def score(b, a):
                    if a == 0:
                        pe.wait_ge(k["k_ready"], b.i + 1)
                    if a >= 2:
                        pe.wait_ge(k["probs_ready"], BT * b.i + (a - 1))
                    pe.matmul(bank[4 + a % 2][:, :], QT[:, a * P:(a + 1) * P], KT,
                              start=True, stop=True).then_inc(k["s_made"], 1)

                def turn(c, g):
                    name = ("even", "odd")[g % 2]
                    if g == 0:
                        pe.wait_ge(k["scaled"], BT * (c.i + 1))
                    for a in range(BT):
                        mm = pe.transpose(chunk(bank[6 + g % 2], a), big[:, c.buf, a, g * P:(g + 1) * P],
                                          ident[:, :])
                    mm.then_inc(k["t_" + name], 1)

                def times_values(c, g):
                    name = ("even", "odd")[g % 2]
                    pe.wait_ge(k["c_" + name], 2 * c.i + (g // 2 + 1))
                    pe.matmul(bank[2][:, :], V[:, c.buf, g, :], PT[:, g % 2, :], start=(g == 0),
                              stop=(g == G - 1)).then_inc(k["av_made"], 1)

                def body(at):
                    new, b, c, old, out = at(1), at(0), at(-1), at(-3), at(-4)
                    if b.live:
                        score(b, 2)
                    if c.live:
                        turn(c, 0)
                        turn(c, 1)
                    if b.live:
                        score(b, 3)
                    if new.live:
                        pe.wait_ge(k["a_normed"], new.i + 1)
                        if due(new.i):
                            pe.wait_ge(k["v_ready"], new.i)
                        for j in range(BT):
                            mm = pe.transpose(chunk(bank[0], j), AN[:, j, :], ident[:, :])
                        mm.then_inc(k["a_turned"], 1)
                    if out.live:
                        pe_rank(pe, out, NB)
                    if c.live:
                        times_values(c, 0)
                        turn(c, 2)
                        times_values(c, 1)
                        turn(c, 3)
                    if old.live:
                        pe_route(pe, old, NB)
                    if new.live:
                        pe.wait_ge(k["a_copied"], new.i + 1)
                        if due(BT * new.i - 1):
                            pe.wait_ge(k["probs_ready"], BT * new.i - 1)
                        pe.matmul(bank[4][:, :], WT4[:, 0, :], AXT, start=True, stop=True)\
                          .then_inc(k["q_made"], 1)
                        if due(BT * new.i):
                            pe.wait_ge(k["probs_ready"], BT * new.i)
                        pe.matmul(bank[5][:, :], WT4[:, 1, :], AXT, start=True, stop=True)\
                          .then_inc(k["k_made"], 1)
                    if old.live:
                        pe_score(pe, old, NB)
                    if c.live:
                        times_values(c, 2)
                    if new.live:
                        score(new, 0)
                        score(new, 1)
                    if c.live:
                        times_values(c, 3)
                    if new.live:
                        pe_bias(bank[0], 0)
                        for j in range(BT):
                            mm = pe.matmul(chunk(bank[0], j), AXT[:, j * P:(j + 1) * P], WT4[:, 2, :],
                                           start=False, stop=(j == BT - 1))
                        mm.then_inc(k["v_made"], 1)
                    if c.live:
                        pe.wait_ge(k["ot_ready"], c.i + 1)
                        pe_bias(bank[3], 1)
                        for j in range(BT):
                            mm = pe.matmul(chunk(bank[3], j), OT[:, j * P:(j + 1) * P], WT4[:, 3, :],
                                           start=False, stop=(j == BT - 1))
                        mm.then_inc(k["proj_made"], 1)
                rolled(pe, NB, 1, 4, body)

            @block.gpsimd
            def _(pool):
                def body(at):
                    ahead, old, out = at(2), at(-3), at(-4)
                    if ahead.live:
                        pool_sum(pool, ahead, 0)
                    if out.live:
                        pool.wait_ge(k["gate_done"], NB + out.i + 1)
                        if due(BT * TOPK * 16 * (NB // 2 + out.uses)):
                            pool.wait_ge(scattered[out.buf], BT * TOPK * 16 * (NB // 2 + out.uses))
                        pool.tensor_tensor(PAY[:, out.buf, 1, :, 0:D], XN[:, out.buf, :, :],
                                           GATE[:, out.buf, :, 1:2].to_broadcast([P, BT, D]), ALU.mult)\
                            .then_inc(k["pay1"], 1)
                        pool_scatter(pool, out, NB)
                    if old.live:
                        pool.wait_ge(k["xt_copied"], NB + old.i + 1)
                        pool.tensor_copy(cut(XTR, W * old.i, W), XT32[:, old.buf, :]).then_inc(k["xt_split"], 1)
                rolled(pool, NB, 2, 4, body)
                for s in scattered:
                    pool.wait_ge(s, BT * TOPK * 16 * NB)

        experts(NT)

        with nc.Block() as block:
            @block.sync
            def _(sp):
                def body(at):
                    b, old = at(0), at(-2)
                    if b.live:
                        load_y(sp, b, NB)
                    if old.live:
                        sp.wait_ge(k["combined"], NB + old.i + 1)
                        if due(16 * old.uses):
                            sp.wait_ge(stored[old.buf], 16 * old.uses)
                        sp.dma_start(out_t[:, BT * old.i:BT * old.i + BT, :] if isinstance(old.i, int)
                                     else out_t[:, ds(BT * old.i, BT), :], x_block(old)).then_inc(stored[old.buf], 16)
                rolled(sp, NB, 0, 2, body)
                for s in stored:
                    sp.wait_ge(s, 16 * NB // 2)

            @block.gpsimd
            def _(pool):
                rolled(pool, NB, 0, 0, lambda at: pool_sum(pool, at(0), NB))

            @block.tensor
            def _(pe):
                def body(at):
                    new, b = at(1), at(0)
                    if new.live:
                        pe_shared_up(pe, new, NB)
                    if b.live:
                        pe_shared_down(pe, b, NB)
                rolled(pe, NB, 1, 0, body)

            @block.scalar
            def _(act):
                def body(at):
                    nxt, new = at(2), at(1)
                    if nxt.live:
                        act_high_kept(act, nxt)
                    if new.live:
                        act_shared(act, new, NB)
                rolled(act, NB, 2, 0, body)

            @block.vector
            def _(dve):
                st = Steps(dve, vec, vec_at[0])

                def body(at):
                    nxt, new, b = at(2), at(1), at(0)
                    if new.live:
                        dve_shared_mul(dve, st, new, NB)
                    if nxt.live:
                        dve_low_kept(dve, st, nxt)
                    if b.live:
                        dve_shared_add(dve, st, b, NB)
                        dve.wait_ge(k["shared_added"], NB + b.i + 1)
                        dve_add_results(dve, st, b, NB)
                rolled(dve, NB, 2, 0, body, st, 0)


_INS = ["L0_attn_batch", "L0_attn_Wq", "L0_attn_bq", "L0_attn_Wk", "L0_attn_bk", "L0_attn_Wv", "L0_attn_bv",
        "L0_attn_Wo", "L0_attn_bo", "L0_ffn_router_DE", "L0_ffn_w_in_shared_FD", "L0_ffn_w_out_shared_DF",
        "L0_ffn_w_swiglu_FD", "L0_ffn_w_in_eDF", "L0_ffn_w_swiglu_eDF", "L0_ffn_w_out_eFD"]


def kernel(**inputs):
    import numpy as np
    import concourse.bacc as bacc
    from concourse.bass_utils import run_bass_kernel_spmd as run

    nc = bacc.Bacc("TRN2", target_bir_lowering=False, num_devices=1)
    arrays, args = {}, []
    for name in _INS:
        a = np.ascontiguousarray(inputs[name])
        arrays[name] = a
        args.append(nc.dram_tensor(name, a.shape, mybir.dt.from_np(a.dtype), kind="ExternalInput").ap())
    shape = arrays["L0_attn_batch"].shape
    args.append(nc.dram_tensor("out", shape, F32, kind="ExternalOutput").ap())
    macaron(nc, *args)
    r = run(nc, [arrays], core_ids=[0])
    return r.results[0]["out"]
```
